# Optimizing a Trainium2 kernel written in Bass

```python
import numpy as np
import jax
import jax.numpy as jnp

def _softmax(x, axis=-1):
    return jax.nn.softmax(x, axis=axis)

def _gelu(x):
    return jax.nn.gelu(x, approximate=True)

def _silu(x):
    return jax.nn.silu(x)

def _sigmoid(x):
    return jax.nn.sigmoid(x)

def _layernorm(x, axis=-1, eps=1e-05):
    m = jnp.mean(x, axis=axis, keepdims=True)
    v = jnp.var(x, axis=axis, keepdims=True)
    return (x - m) / jnp.sqrt(v + eps)

def _scatter_add(tgt, idx, src, axis=0):
    return tgt.at[idx].add(src)

def _segment_sum(src, seg, n):
    return jax.ops.segment_sum(src, seg, n)
kernel_name = 'mk_adaln_attn_ffn_d1_seqx_r4_9fc849'

def setup_inputs(seed: int=0):
    np.random.seed(seed)
    _w = jnp.asarray

    def _rec_inputs():
        import jax
        import jax.numpy as jnp
        _rk = jax.random.key(seed)
        x = -0.0003929 + 0.9999 * jax.random.normal(jax.random.fold_in(_rk, 1), (8, 512, 256), jnp.float32)
        _lenS = 512 - jax.random.randint(jax.random.fold_in(_rk, 7), (8,), 0, max(1, 512 // 4) + 1, jnp.int32)
        _lenS2 = 512 - jax.random.randint(jax.random.fold_in(_rk, 8), (8,), 0, max(1, 512 // 4) + 1, jnp.int32)
        itok_B_0_7 = jax.random.randint(jax.random.fold_in(_rk, 11), (8,), 0, 8, jnp.int32)
        return (x, itok_B_0_7)
    x, itok_B_0_7 = _rec_inputs()

    def _L0_cond_setup():
        import jax, jax.numpy as jnp
        import numpy as np
        S, O, H = (8, 256, 256)
        B, N = (32, 128)
        key = jax.random.key(seed)
        k1, k2, k3, k4 = jax.random.split(key, 4)
        x = jax.random.normal(k1, (B, N, H), dtype=jnp.float32)
        subject_id = jax.random.randint(k2, (B,), 0, S)
        wbound = jnp.sqrt(2.0 / 6.0) * jnp.sqrt(3.0 / H)
        weight = jax.random.uniform(k3, (S, O, H), minval=-wbound, maxval=wbound, dtype=jnp.float32)
        bbound = 1.0 / jnp.sqrt(H)
        bias = jax.random.uniform(k4, (S, O), minval=-bbound, maxval=bbound, dtype=jnp.float32)
        return {'x': x, 'subject_id': subject_id, 'weight': weight, 'bias': bias}
    _L0_cond_all = _L0_cond_setup()
    _L0_cond_in = {k: v for k, v in _L0_cond_all.items() if k in ('weight', 'bias')}
    del _L0_cond_all

    def _L0_attn_setup():
        import jax, jax.numpy as jnp
        import numpy as np
        D_MODEL = 256
        N_HEADS = 16
        D_HEAD = D_MODEL // N_HEADS
        SEQ = 1024
        BATCH = 1
        key = jax.random.key(seed)
        kx, kq, kk, kv, ko = jax.random.split(key, 5)
        scale = (1.0 / D_MODEL) ** 0.5
        return {'x': jax.random.normal(kx, (BATCH, SEQ, D_MODEL), dtype=jnp.float32), 'W_Q': jax.random.normal(kq, (D_MODEL, D_MODEL), dtype=jnp.float32) * scale, 'W_K': jax.random.normal(kk, (D_MODEL, D_MODEL), dtype=jnp.float32) * scale, 'W_V': jax.random.normal(kv, (D_MODEL, D_MODEL), dtype=jnp.float32) * scale, 'W_o': jax.random.normal(ko, (D_MODEL, D_MODEL), dtype=jnp.float32) * scale}
    _L0_attn_all = _L0_attn_setup()
    _L0_attn_in = {k: v for k, v in _L0_attn_all.items() if k in ('W_Q', 'W_K', 'W_V', 'W_o')}
    del _L0_attn_all

    def _L0_cond2_setup():
        import jax, jax.numpy as jnp
        import numpy as np
        B, S, D, F = (32, 128, 256, 1024)
        R_COMMON, R_DOMAIN, E = (16, 16, 8)
        ALPHA = 2.0

        def _expert_lora(x, expert_ids, Wa, Wb):
            Ab = Wa[expert_ids]
            Bb = Wb[expert_ids]
            low = jnp.einsum('bsd,brd->bsr', x, Ab)
            return ALPHA * jnp.einsum('bsr,bor->bso', low, Bb)
        key = jax.random.key(seed)
        ks = jax.random.split(key, 12)
        sd = lambda k, shape: jax.random.normal(k, shape, dtype=jnp.float32) * (1.0 / np.sqrt(shape[-1]))
        return {'hidden_states': jax.random.normal(ks[0], (B, S, D), dtype=jnp.float32), 'expert_ids': jax.random.randint(ks[1], (B,), 0, E, dtype=jnp.int32), 'wi': sd(ks[2], (F, D)), 'wo': sd(ks[3], (D, F)), 'common_wi_a': sd(ks[4], (R_COMMON, D)), 'common_wi_b': sd(ks[5], (F, R_COMMON)), 'common_wo_a': sd(ks[6], (R_COMMON, F)), 'common_wo_b': sd(ks[7], (D, R_COMMON)), 'experts_wi_a': sd(ks[8], (E, R_DOMAIN, D)), 'experts_wi_b': sd(ks[9], (F, R_DOMAIN)) * jnp.ones((E, 1, 1)) * 0.0 + sd(ks[9], (E, F, R_DOMAIN)), 'experts_wo_a': sd(ks[10], (E, R_DOMAIN, F)), 'experts_wo_b': sd(ks[11], (E, D, R_DOMAIN))}
    _L0_cond2_all = _L0_cond2_setup()
    _L0_cond2_in = {k: v for k, v in _L0_cond2_all.items() if k in ('wi', 'wo', 'common_wi_a', 'common_wi_b', 'common_wo_a', 'common_wo_b', 'experts_wi_a', 'experts_wi_b', 'experts_wo_a', 'experts_wo_b')}
    del _L0_cond2_all

    def _L0_ffn_setup():
        import jax, jax.numpy as jnp
        import numpy as np
        B, S, E, H, NE, TOP_K = (4, 512, 256, 512, 8, 2)
        key = jax.random.key(seed)
        ks = jax.random.split(key, 5)
        s = 0.02
        return {'x': jax.random.normal(ks[0], (B, S, E), jnp.float32), 'w1': jax.random.normal(ks[1], (NE, E, H), jnp.float32) * s, 'b1': jnp.zeros((NE, H), jnp.float32), 'w2': jax.random.normal(ks[2], (NE, H, H), jnp.float32) * s, 'b2': jnp.zeros((NE, H), jnp.float32), 'w3': jax.random.normal(ks[3], (NE, H, E), jnp.float32) * s, 'b3': jnp.zeros((NE, E), jnp.float32), 'gate_w': jax.random.normal(ks[4], (E, NE), jnp.float32) * s, 'gate_b': jnp.zeros((NE,), jnp.float32)}
    _L0_ffn_all = _L0_ffn_setup()
    _L0_ffn_in = {k: v for k, v in _L0_ffn_all.items() if k in ('w1', 'b1', 'w2', 'b2', 'w3', 'b3', 'gate_w', 'gate_b')}
    del _L0_ffn_all
    return {'x': x, 'itok_B_0_7': itok_B_0_7, 'L0_cond_weight': _L0_cond_in['weight'], 'L0_cond_bias': _L0_cond_in['bias'], 'L0_attn_W_Q': _L0_attn_in['W_Q'], 'L0_attn_W_K': _L0_attn_in['W_K'], 'L0_attn_W_V': _L0_attn_in['W_V'], 'L0_attn_W_o': _L0_attn_in['W_o'], 'L0_cond2_wi': _L0_cond2_in['wi'], 'L0_cond2_wo': _L0_cond2_in['wo'], 'L0_cond2_common_wi_a': _L0_cond2_in['common_wi_a'], 'L0_cond2_common_wi_b': _L0_cond2_in['common_wi_b'], 'L0_cond2_common_wo_a': _L0_cond2_in['common_wo_a'], 'L0_cond2_common_wo_b': _L0_cond2_in['common_wo_b'], 'L0_cond2_experts_wi_a': _L0_cond2_in['experts_wi_a'], 'L0_cond2_experts_wi_b': _L0_cond2_in['experts_wi_b'], 'L0_cond2_experts_wo_a': _L0_cond2_in['experts_wo_a'], 'L0_cond2_experts_wo_b': _L0_cond2_in['experts_wo_b'], 'L0_ffn_w1': _L0_ffn_in['w1'], 'L0_ffn_b1': _L0_ffn_in['b1'], 'L0_ffn_w2': _L0_ffn_in['w2'], 'L0_ffn_b2': _L0_ffn_in['b2'], 'L0_ffn_w3': _L0_ffn_in['w3'], 'L0_ffn_b3': _L0_ffn_in['b3'], 'L0_ffn_gate_w': _L0_ffn_in['gate_w'], 'L0_ffn_gate_b': _L0_ffn_in['gate_b']}

def reference(x, itok_B_0_7, L0_cond_weight, L0_cond_bias, L0_attn_W_Q, L0_attn_W_K, L0_attn_W_V, L0_attn_W_o, L0_cond2_wi, L0_cond2_wo, L0_cond2_common_wi_a, L0_cond2_common_wi_b, L0_cond2_common_wo_a, L0_cond2_common_wo_b, L0_cond2_experts_wi_a, L0_cond2_experts_wi_b, L0_cond2_experts_wo_a, L0_cond2_experts_wo_b, L0_ffn_w1, L0_ffn_b1, L0_ffn_w2, L0_ffn_b2, L0_ffn_w3, L0_ffn_b3, L0_ffn_gate_w, L0_ffn_gate_b):
    import jax
    import jax.numpy as jnp

    def _L0_cond_ref(x, subject_id, weight, bias):
        import jax, jax.numpy as jnp
        import numpy as np
        S, O, H = (8, 256, 256)
        B, N = (32, 128)
        W = weight[subject_id]
        b = bias[subject_id]
        y = jnp.einsum('bnh,boh->bno', x, W) + b[:, None, :]
        return y

    def _L0_attn_ref(x, W_Q, W_K, W_V, W_o):
        import jax, jax.numpy as jnp
        import numpy as np
        D_MODEL = 256
        N_HEADS = 16
        D_HEAD = D_MODEL // N_HEADS
        SEQ = 1024
        BATCH = 1
        B, S, _ = x.shape

        def heads(w):
            return (x @ w).reshape(B, S, N_HEADS, D_HEAD).transpose(0, 2, 1, 3)
        Q, K, V = (heads(W_Q), heads(W_K), heads(W_V))
        scores = jnp.einsum('bhqd,bhkd->bhqk', Q, K) / D_HEAD ** 0.5
        causal = jnp.triu(jnp.full((S, S), -jnp.inf, dtype=scores.dtype), k=1)
        scores = scores + causal
        probs = jax.nn.softmax(scores, axis=-1)
        out = jnp.einsum('bhqk,bhkd->bhqd', probs, V)
        out = out.transpose(0, 2, 1, 3).reshape(B, S, D_MODEL)
        return out @ W_o

    def _L0_cond2_ref(hidden_states, expert_ids, wi, wo, common_wi_a, common_wi_b, common_wo_a, common_wo_b, experts_wi_a, experts_wi_b, experts_wo_a, experts_wo_b):
        import jax, jax.numpy as jnp
        import numpy as np
        B, S, D, F = (32, 128, 256, 1024)
        R_COMMON, R_DOMAIN, E = (16, 16, 8)
        ALPHA = 2.0

        def _expert_lora(x, expert_ids, Wa, Wb):
            Ab = Wa[expert_ids]
            Bb = Wb[expert_ids]
            low = jnp.einsum('bsd,brd->bsr', x, Ab)
            return ALPHA * jnp.einsum('bsr,bor->bso', low, Bb)
        x = hidden_states
        hidden_i = jnp.einsum('bsd,fd->bsf', x, wi)
        hidden_i += ALPHA * jnp.einsum('bsr,fr->bsf', jnp.einsum('bsd,rd->bsr', x, common_wi_a), common_wi_b)
        hidden_i += _expert_lora(x, expert_ids, experts_wi_a, experts_wi_b)
        hidden_i = jax.nn.relu(hidden_i)
        hidden_o = jnp.einsum('bsf,df->bsd', hidden_i, wo)
        hidden_o += ALPHA * jnp.einsum('bsr,dr->bsd', jnp.einsum('bsf,rf->bsr', hidden_i, common_wo_a), common_wo_b)
        hidden_o += _expert_lora(hidden_i, expert_ids, experts_wo_a, experts_wo_b)
        return hidden_o

    def _L0_ffn_ref(x, w1, b1, w2, b2, w3, b3, gate_w, gate_b):
        import jax, jax.numpy as jnp
        import numpy as np
        B, S, E, H, NE, TOP_K = (4, 512, 256, 512, 8, 2)
        gate_weights = jax.nn.softmax(x @ gate_w + gate_b, axis=-1)
        topk_vals, topk_idx = jax.lax.top_k(gate_weights, TOP_K)
        h = jax.nn.gelu(jnp.einsum('bse,neh->bsnh', x, w1) + b1, approximate=False)
        h = jax.nn.gelu(jnp.einsum('bsnh,nhk->bsnk', h, w2) + b2, approximate=False)
        expert_out = jnp.einsum('bsnh,nhe->bsne', h, w3) + b3
        gathered = jnp.take_along_axis(expert_out, topk_idx[..., None], axis=2)
        return jnp.sum(topk_vals[..., None] * gathered, axis=2)
    x = x + _L0_attn_ref(_L0_cond_ref(x, itok_B_0_7, L0_cond_weight, L0_cond_bias), L0_attn_W_Q, L0_attn_W_K, L0_attn_W_V, L0_attn_W_o)
    x = x + _L0_ffn_ref(_L0_cond2_ref(x, itok_B_0_7, L0_cond2_wi, L0_cond2_wo, L0_cond2_common_wi_a, L0_cond2_common_wi_b, L0_cond2_common_wo_a, L0_cond2_common_wo_b, L0_cond2_experts_wi_a, L0_cond2_experts_wi_b, L0_cond2_experts_wo_a, L0_cond2_experts_wo_b), L0_ffn_w1, L0_ffn_b1, L0_ffn_w2, L0_ffn_b2, L0_ffn_w3, L0_ffn_b3, L0_ffn_gate_w, L0_ffn_gate_b)
    return x

_drawn_inputs = setup_inputs


def setup_inputs(seed=0):
    import zlib

    import numpy as np

    out = dict(_drawn_inputs(seed))
    spreads = {'L0_ffn_b1': (0.0, 0.8),
     'L0_ffn_b2': (0.0, 0.386),
     'L0_ffn_b3': (0.0, 0.1),
     'L0_ffn_gate_b': (0.0, 0.679)}
    factors = {}
    for name, (base, spread) in spreads.items():
        noise = np.random.default_rng([zlib.crc32(name.encode()), seed]).standard_normal(out[name].shape)
        drawn = base * np.exp(spread * noise) if base else spread * noise
        out[name] = jnp.asarray(drawn.astype(out[name].dtype))
    for name, factor in factors.items():
        out[name] = (out[name] * factor).astype(out[name].dtype)
    return out
```

```python
from contextlib import ExitStack

import concourse.bass as bass
from concourse import mybir

F32 = mybir.dt.float32
F32R = mybir.dt.float32r
BF16 = mybir.dt.bfloat16
I32 = mybir.dt.int32
U32 = mybir.dt.uint32
ALU = mybir.AluOpType
ACT = mybir.ActivationFunctionType
AX = mybir.AxisListType

P = 128
B, S, D = 8, 512, 256
KD = D // P
TB = S // P
HEADS, DH = 16, 16
STRIP = 32
HC = HEADS * STRIP // P
F = 1024
KF = F // P
R = 16
LORA = D + F + F + D
NE = 8
H = 512
KH = H // P
NT = B * TB
ROW = D + NE
TILES = (2 * B * S + NE * (P - 1)) // P
BIG = 1.0e30
UNITS = TB * HEADS
T_LAG, PV_LAG, OT_LAG = 3, 5, 8


def units_at(step):
    def unit(n):
        return n if 0 <= n < UNITS else None
    n_ot = step - OT_LAG
    ot = n_ot // HEADS if n_ot >= 0 and n_ot % HEADS == HEADS - 1 else None
    return unit(step), unit(step - T_LAG), unit(step - PV_LAG), ot


def psum_plan():
    ring, tring = [0, 1, 2, 3], [4, 5]
    uses = [0] * 8
    turn = {"ring": 0, "tring": 0}
    plan = {}

    def take(name, kind):
        banks = ring if kind == "ring" else tring
        bank = banks[turn[kind] % len(banks)]
        turn[kind] += 1
        plan[name] = (bank, uses[bank])
        uses[bank] += 1

    for o in range(KD):
        take(("cond", o), "ring")
    for n in range(2 * KD):
        take(("fold_i", n), "ring")
    for c in range(HC):
        take(("q", c), "ring")
        take(("k", c), "ring")
    for t in range(TB // 2):
        take(("v", t), "ring")
    for n in range(KF // 2):
        take(("fold_o", n), "ring")
    for step in range(UNITS + OT_LAG):
        s, t, pv, ot = units_at(step)
        if s is not None:
            take(("s", s), "ring")
        if t is not None:
            take(("t", t), "tring")
        if pv is not None and pv % HEADS == 0:
            bank = 6 + (pv // HEADS) % 2
            plan[("pv", pv // HEADS)] = (bank, uses[bank])
            uses[bank] += 1
        if ot is not None:
            take(("ot", ot), "tring")
    for o in range(KD):
        take(("x1t", o), "ring")
    for t in range(TB // 2):
        take(("x1", t), "ring")
    for j in range(KF):
        take(("hid", j), "ring")
    for t in range(TB // 2):
        take(("h", t), "ring")
    for k in range(KD):
        take(("ht", k), "ring")
    take(("gate", 0), "ring")
    return plan, uses


def build_kernel(nc, xT, x_cond_w, x_cond_b, itok, wq, wk, wv, wo, wi_t, wo_t, lora_c, lora_e,
                 gate_w, gate_b, w1, w2, w3, b1, b2, b3, ident, maskd, tri, low, iota_r, iota_t,
                 tok, thr, out):
    plan, uses = psum_plan()
    hrows = nc.dram_tensor("hrows", [B * S, ROW], F32, kind="Internal").ap()
    out_rows = out.rearrange("b s d -> (b s) d")

    outer = ExitStack()
    part_a = ExitStack()
    with outer:
        def sb(name, shape, dt, ctx=outer):
            return ctx.enter_context(nc.sbuf_tensor(name, shape, dt))

        def sem(name):
            return outer.enter_context(nc.semaphore(name))

        bank = [outer.enter_context(nc.psum_tensor(f"bank{i}", [P, 512], F32)) for i in range(8)]

        id_f = sb("id_f", [P, P], F32)
        id_b = sb("id_b", [P, P], BF16)
        mask_b = sb("mask_b", [P, P], BF16)
        mask_f = sb("mask_f", [P, P], F32)
        itok_sb = sb("itok_sb", [1, B], I32)
        low_sb = sb("low_sb", [P, 1], F32)
        gb_sb = sb("gb_sb", [P, NE], F32)
        logits = sb("logits", [P, NT, NE], F32)
        w1_sb = sb("w1_sb", [P, NE, KD, H], F32)
        b3_sb = sb("b3_sb", [P, NE, D], F32)

        x_in = sb("x_in", [P, KD, S], F32, part_a)
        x_res = sb("x_res", [P, KD, S], F32, part_a)
        wc_sb = sb("wc_sb", [P, KD, D], F32, part_a)
        bc_sb = sb("bc_sb", [P, KD], F32, part_a)
        cond = sb("cond", [P, KD, S], F32, part_a)
        wq_raw = sb("wq_raw", [P, KD, HC * P], F32, part_a)
        wk_sb = sb("wk_sb", [P, KD, HC * P], F32, part_a)
        wv_sb = sb("wv_sb", [P, KD, D], F32, part_a)
        wo_sb = sb("wo_sb", [P, KD, D], F32, part_a)
        q_sb = sb("q_sb", [P, HC, S], F32R, part_a)
        kh_sb = sb("kh_sb", [P, HC, S], F32R, part_a)
        kl_sb = sb("kl_sb", [P, HC, S], F32R, part_a)
        q_hi = sb("q_hi", [P, S], F32R, part_a)
        v_sb = sb("v_sb", [P, TB, D], F32, part_a)
        probs = sb("probs", [P, 4, S], F32, part_a)
        probs_t = sb("probs_t", [P, 4, S], F32, part_a)
        nmax = sb("nmax", [P, 8], F32, part_a)
        rsum = sb("rsum", [P, 2, HEADS], F32, part_a)
        rinv = sb("rinv", [P, HEADS], F32, part_a)
        o_sb = sb("o_sb", [P, 2, D], F32, part_a)
        ot_sb = sb("ot_sb", [P, KD, S], F32, part_a)
        x1t = sb("x1t", [P, KD, S], F32, part_a)
        x1_sb = sb("x1_sb", [P, TB, D], F32, part_a)
        wi_base = sb("wi_base", [P, KD, F], F32, part_a)
        wi_eff = sb("wi_eff", [P, KD, F], F32, part_a)
        wf_base = sb("wf_base", [P, KF, D], F32, part_a)
        wf_eff = sb("wf_eff", [P, KF, D], F32, part_a)
        lora = sb("lora", [2 * R, LORA], F32, part_a)
        hid = sb("hid", [P, KF, S], F32, part_a)
        h_sb = sb("h_sb", [P, TB, ROW], F32, part_a)
        ht_sb = sb("ht_sb", [P, KD, S], F32, part_a)
        gw_sb = sb("gw_sb", [P, KD, NE], F32, part_a)
        glog = sb("glog", [P, TB, NE], F32, part_a)
        gmax = sb("gmax", [P, TB], F32, part_a)
        gexp = sb("gexp", [P, TB, NE], F32, part_a)
        gsum = sb("gsum", [P, TB], F32, part_a)
        ginv = sb("ginv", [P, TB], F32, part_a)
        part_a.close()

        w2_sb = sb("w2_sb", [P, NE, KH, H], F32)
        w3_sb = sb("w3_sb", [P, NE, KH, D], F32)
        b1_sb = sb("b1_sb", [P, NE, H], F32)
        b2_sb = sb("b2_sb", [P, NE, H], F32)
        route = ExitStack()
        etab = sb("etab", [1, TILES], I32)
        gather_id = sb("gather_id", [P, TILES], U32)
        scatter_id = sb("scatter_id", [P, TILES], U32)
        with route:
            tri_f = sb("tri_f", [P, P], F32, route)
            tri_sb = sb("tri_sb", [P, P], BF16, route)
            ones_b = sb("ones_b", [P, P], BF16, route)
            iota_r_sb = sb("iota_r_sb", [P, P], F32, route)
            iota_t_sb = sb("iota_t_sb", [P, TILES], F32, route)
            tok_sb = sb("tok_sb", [P, NT, 2], F32, route)
            thr_sb = sb("thr_sb", [P, NT * 2], F32, route)
            m1 = sb("m1", [P, NT], F32, route)
            rk = sb("rk", [P, NT, NE], F32, route)
            lg2 = sb("lg2", [P, NT, NE], F32, route)
            hot = [sb(f"hot{c}", [P, NT, NE], F32, route) for c in range(2)]
            hots = sb("hots", [P, NT, NE], BF16, route)
            run = [sb(f"run{c}", [P, NT, NE], F32, route) for c in range(2)]
            pre = sb("pre", [P, NT, NE], F32, route)
            cnt = sb("cnt", [P, NE], F32, route)
            cmpt = sb("cmpt", [P, NE, NT * 2], F32, route)
            ntile = sb("ntile", [P, NE], F32, route)
            tbase = sb("tbase", [P, NE + 1], F32, route)
            slot = sb("slot", [P, NT], F32, route)
            s_r = sb("s_r", [P, 2, NT], F32, route)
            s_j = sb("s_j", [P, 2, NT], F32, route)
            s_i = sb("s_i", [P, 2, NT], I32, route)
            hit_r = sb("hit_r", [P, NT, P], BF16, route)
            hit_j = sb("hit_j", [P, NT // 4, TILES], F32, route)
            hit_v = sb("hit_v", [P, NT // 4, 2, TILES], BF16, route)
            ids_f = sb("ids_f", [P, TILES], F32, route)
            ids_g = sb("ids_g", [P, TILES], F32, route)
            etab_f = sb("etab_f", [1, TILES], F32, route)
            eacc = [sb(f"eacc{c}", [1, TILES], F32, route) for c in range(2)]
        xg = sb("xg", [P, ROW], F32)
        xgt = sb("xgt", [P, KD, P], F32)
        gid = sb("gid", [P, 1], U32)
        sid = sb("sid", [P, 1], U32)
        wsel = sb("wsel", [P, TILES], F32)
        z1 = sb("z1", [P, H], F32)
        z2 = sb("z2", [P, H], F32)
        g1 = sb("g1", [P, H], F32)
        g2 = sb("g2", [P, H], F32)
        g1t = sb("g1t", [P, KH, P], F32)
        g2t = sb("g2t", [P, KH, P], F32)
        y0 = sb("y0", [P, D], F32)
        y_sb = sb("y_sb", [P, D], F32)

        full = [sem(f"bank{i}_filled") for i in range(8)]
        free = [sem(f"bank{i}_drained") for i in range(8)]
        s_const = sem("s_const")
        s_mid = sem("s_mid")
        s_in = sem("s_in")
        s_xres = sem("s_xres")
        s_lora = sem("s_lora")
        s_x1out = sem("s_x1out")
        s_hout = sem("s_hout")
        s_prep = sem("s_prep")
        s_idb = sem("s_idb")
        s_hi = sem("s_hi")
        s_max = sem("s_max")
        s_chain = sem("s_chain")
        s_oready = sem("s_oready")
        s_gneg = sem("s_gneg")
        s_gexp = sem("s_gexp")
        s_gchain = sem("s_gchain")
        s_hdone = sem("s_hdone")
        s_rchain = sem("s_rchain")
        s_rconst = sem("s_rconst")
        s_ohot = sem("s_ohot")
        s_cnts = sem("s_cnts")
        s_hit = sem("s_hit")
        s_hitu = sem("s_hitu")
        s_route = sem("s_route")
        s_w23 = sem("s_w23")
        s_w1 = sem("s_w1")
        s_gid = sem("s_gid")
        s_xg = sem("s_xg")
        s_wsel = sem("s_wsel")
        s_z1 = sem("s_z1")
        s_g1 = sem("s_g1")
        s_z2 = sem("s_z2")
        s_g2 = sem("s_g2")
        s_y = sem("s_y")
        s_sid = sem("s_sid")
        s_tick = sem("s_tick")
        s_add = sem("s_add")
        N_CONST, N_MID, N_RC = 12, 8, 5
        CHAIN = TB + 1
        BX, BT1, BT2, BL1, BL2, BL3 = 0, 1, 2, 3, 4, 5

        block = outer.enter_context(nc.Block())

        def filled(eng, name, b):
            i, k = plan[name]
            eng.wait_ge(full[i], b * uses[i] + (k + 1))

        def drained(eng, name, b):
            i, k = plan[name]
            eng.wait_ge(free[i], b * uses[i] + (k + 2))

        def vacant(eng, name, b, after=()):
            least = {plan[name][0]: plan[name][1] + 1}
            for other in after:
                i, k = plan[other]
                least[i] = max(least.get(i, 0), k + 2)
            for i, v in least.items():
                eng.wait_ge(free[i], b * uses[i] + v)

        def at(name):
            return bank[plan[name][0]]

        def done(ins, name):
            ins.then_inc(full[plan[name][0]], 1)

        def taken(ins, name):
            ins.then_inc(free[plan[name][0]], 1)

        before_b = [B * uses[i] for i in range(8)]
        PRE_BANK, TOT_BANK, ID_BANK = 0, 1, 2
        b_uses = [1, 1, 1, 0, 0, 0, 0, 0]
        before_c = [before_b[i] + b_uses[i] for i in range(8)]

        @block.sync
        def _(sp):
            sp.dma_start(itok_sb[:, :], itok).then_inc(s_const, 16)
            sp.dma_start(wq_raw[:, :, :], wq).then_inc(s_const, 16)
            sp.dma_start(wk_sb[:, :, :], wk).then_inc(s_const, 16)
            sp.dma_start(wv_sb[:, :, :], wv).then_inc(s_const, 16)
            sp.dma_start(wo_sb[:, :, :], wo).then_inc(s_const, 16)
            sp.dma_start(wi_base[:, :, :], wi_t).then_inc(s_const, 16)
            sp.dma_start(wf_base[:, :, :], wo_t).then_inc(s_const, 16)
            sp.dma_start(lora[0:R, :], lora_c).then_inc(s_const, 16)
            sp.dma_start(id_f[:, :], ident).then_inc(s_const, 16)
            sp.dma_start(mask_f[:, :], maskd).then_inc(s_const, 16)
            sp.dma_start(low_sb[:, :], low).then_inc(s_const, 16)
            sp.dma_start(gw_sb[:, :, :], gate_w).then_inc(s_const, 16)
            sp.wait_ge(s_const, 16 * N_CONST)

            def expert_of(b):
                return sp.value_load(itok_sb[0:1, bass.ds(b, 1)], min_val=0, max_val=NE - 1)

            def load_in(b, e):
                sp.dma_start(x_in[:, :, :], xT[bass.ds(b, 1), :, :, :].rearrange("o p k t -> (o p) k t")
                             ).then_inc(s_in, 16)
                sp.dma_start(wc_sb[:, :, :], x_cond_w[bass.ds(e, 1), :, :, :].rearrange("o p k t -> (o p) k t")
                             ).then_inc(s_in, 16)
                sp.dma_start(bc_sb[:, :], x_cond_b[bass.ds(e, 1), :, :].rearrange("o p k -> (o p) k")
                             ).then_inc(s_in, 16)

            def load_lora(e):
                sp.dma_start(lora[R:2 * R, :], lora_e[bass.ds(e, 1), :, :].rearrange("o r n -> (o r) n")
                             ).then_inc(s_lora, 16)

            def load_res(b):
                sp.dma_start(x_res[:, :, :], xT[bass.ds(b, 1), :, :, :].rearrange("o p k t -> (o p) k t")
                             ).then_inc(s_xres, 16)

            def value(b, name, more):
                i, k = plan[name]
                return sp.snap(b * uses[i] + (k + more)) if not isinstance(b, int) else b * uses[i] + k + more

            def store(b, v_x1, v_hdone):
                for t2 in range(TB // 2):
                    sp.wait_ge(free[plan[("x1", t2)][0]], v_x1[t2])
                    sp.sem_inc(s_tick, 1)
                sp.dma_start(out[bass.ds(b, 1), :, :].rearrange("o (t p) d -> p (o t) d", p=P),
                             x1_sb[:, :, :]).then_inc(s_x1out, 16)
                sp.wait_ge(s_hdone, v_hdone)
                sp.sem_inc(s_tick, 1)
                sp.dma_start(hrows[bass.ds(b * S, S), :].rearrange("(t p) d -> p t d", p=P),
                             h_sb[:, :, :]).then_inc(s_hout, 16)

            e0 = expert_of(0)
            load_in(0, e0)
            load_lora(e0)
            load_res(0)
            sp.dma_start(gb_sb[:, :], gate_b.partition_broadcast(P)).then_inc(s_mid, 16)
            sp.dma_start(b3_sb[:, :, :].rearrange("p e d -> p (e d)"), b3.partition_broadcast(P)).then_inc(s_mid, 16)
            for e in range(NE):
                sp.dma_start(w1_sb[:, e, :, :], w1[e]).then_inc(s_w1, 16)
            with sp.Fori(0, B - 1) as b:
                b1_ = sp.snap(b + 1)
                e = expert_of(b1_)
                v_read = value(b, ("cond", KD - 1), 1)
                v_cond = [value(b, ("cond", o), 2) for o in range(KD)]
                v_fold = value(b, ("fold_o", KF // 2 - 1), 1)
                v_x1t = [value(b, ("x1t", o), 2) for o in range(KD)]
                v_x1 = [value(b, ("x1", t2), 2) for t2 in range(TB // 2)]
                sp.wait_ge(full[plan[("cond", KD - 1)][0]], v_read)
                sp.sem_inc(s_tick, 1)
                for o in range(KD):
                    sp.wait_ge(free[plan[("cond", o)][0]], v_cond[o])
                    sp.sem_inc(s_tick, 1)
                load_in(b1_, e)
                sp.wait_ge(full[plan[("fold_o", KF // 2 - 1)][0]], v_fold)
                sp.sem_inc(s_tick, 1)
                load_lora(e)
                for o in range(KD):
                    sp.wait_ge(free[plan[("x1t", o)][0]], v_x1t[o])
                    sp.sem_inc(s_tick, 1)
                load_res(b1_)
                store(b, v_x1, b1_)
            store(B - 1, [value(B - 1, ("x1", t2), 2) for t2 in range(TB // 2)], B)
            sp.wait_ge(s_x1out, 16 * B + 1)
            sp.wait_ge(s_hout, 16 * B + 1)
            for i in range(8):
                sp.wait_ge(full[i], before_b[i])
                sp.wait_ge(free[i], before_b[i] + 1)
            sp.dma_start(tri_f[:, :], tri).then_inc(s_rconst, 16)
            sp.dma_start(iota_r_sb[:, :], iota_r).then_inc(s_rconst, 16)
            sp.dma_start(iota_t_sb[:, :], iota_t).then_inc(s_rconst, 16)
            sp.dma_start(tok_sb[:, :, :], tok).then_inc(s_rconst, 16)
            sp.dma_start(thr_sb[:, :], thr).then_inc(s_rconst, 16)
            sp.dma_start(b1_sb[:, :, :].rearrange("p e d -> p (e d)"), b1.partition_broadcast(P)).then_inc(s_w23, 16)
            sp.dma_start(b2_sb[:, :, :].rearrange("p e d -> p (e d)"), b2.partition_broadcast(P)).then_inc(s_w23, 16)
            for e in range(NE):
                sp.dma_start(w2_sb[:, e, :, :], w2[e]).then_inc(s_w23, 16)
                sp.dma_start(w3_sb[:, e, :, :], w3[e]).then_inc(s_w23, 16)
            sp.wait_ge(s_add, 16 * TILES)

        @block.tensor
        def _(pe):
            for i in range(8):
                pe.sem_inc(free[i], 1)

            def mm(*a, **k):
                return nc.tensor.matmul(*a, **k)

            def batch(b):
                pe.wait_ge(s_in, b * 48 + 48)
                for o in range(KD):
                    n = ("cond", o)
                    vacant(pe, n, b)
                    for k in range(KD):
                        ins = mm(at(n)[:, :], wc_sb[:, k, o * P:(o + 1) * P], x_in[:, k, :],
                                 start=(k == 0), stop=(k == KD - 1))
                    done(ins, n)
                pe.wait_ge(s_lora, b * 16 + 16)
                for n4 in range(2 * KD):
                    n = ("fold_i", n4)
                    k, fh = n4 // 2, n4 % 2
                    vacant(pe, n, b)
                    done(mm(at(n)[:, :], lora[:, k * P:(k + 1) * P], lora[:, D + fh * 512:D + (fh + 1) * 512],
                            start=True, stop=True), n)
                for c in range(HC):
                    for what, w in (("q", wq_raw), ("k", wk_sb)):
                        n = (what, c)
                        vacant(pe, n, b, [("cond", o) for o in range(KD)] if n == ("q", 0) else ())
                        for k in range(KD):
                            ins = mm(at(n)[:, :], w[:, k, c * P:(c + 1) * P], cond[:, k, :],
                                     start=(k == 0), stop=(k == KD - 1))
                        done(ins, n)
                for t2 in range(TB // 2):
                    n = ("v", t2)
                    vacant(pe, n, b)
                    for u in range(2):
                        t = 2 * t2 + u
                        for k in range(KD):
                            ins = mm(at(n)[:, u * D:(u + 1) * D], cond[:, k, t * P:(t + 1) * P], wv_sb[:, k, :],
                                     start=(k == 0), stop=(k == KD - 1))
                    done(ins, n)
                for n4 in range(KF // 2):
                    n = ("fold_o", n4)
                    vacant(pe, n, b)
                    for u in range(2):
                        j = 2 * n4 + u
                        ins = mm(at(n)[:, u * D:(u + 1) * D], lora[:, D + F + j * P:D + F + (j + 1) * P],
                                 lora[:, D + 2 * F:D + 2 * F + D], start=True, stop=True)
                    done(ins, n)
                qkv = [(w, c) for c in range(HC) for w in "qk"] + [("v", t2) for t2 in range(TB // 2)]
                for step in range(UNITS + OT_LAG):
                    s, t, pv, ot = units_at(step)
                    if s is not None:
                        i, h = divmod(s, HEADS)
                        c, r = h // 4, STRIP * (h % 4)
                        n = ("s", s)
                        w = (i + 1) * P
                        vacant(pe, n, b, qkv if s == 0 else ())
                        q = q_sb[r:r + STRIP, c, i * P:(i + 1) * P]
                        mm(at(n)[:, 0:w], q, kh_sb[r:r + STRIP, c, 0:w], start=True, stop=False)
                        mm(at(n)[:, w - P:w], id_b[:, :], mask_b[:, :], start=False, stop=False,
                           skip_group_check=True)
                        done(mm(at(n)[:, 0:w], q, kl_sb[r:r + STRIP, c, 0:w], start=False, stop=True), n)
                    if t is not None:
                        i = t // HEADS
                        n = ("t", t)
                        vacant(pe, n, b, [("s", t)])
                        for kb in range(i + 1):
                            ins = nc.tensor.transpose(at(n)[:, kb * P:(kb + 1) * P],
                                                      probs[:, t % 4, kb * P:(kb + 1) * P], id_f[:, :])
                        done(ins, n)
                    if pv is not None:
                        i, h = divmod(pv, HEADS)
                        n = ("pv", i)
                        if h == 0:
                            vacant(pe, n, b, [("t", pv)])
                        else:
                            drained(pe, ("t", pv), b)
                        for kb in range(i + 1):
                            ins = mm(at(n)[:, h * DH:(h + 1) * DH], probs_t[:, pv % 4, kb * P:(kb + 1) * P],
                                     v_sb[:, kb, h * DH:(h + 1) * DH], start=(kb == 0), stop=(kb == i))
                        if h == HEADS - 1:
                            done(ins, n)
                    if ot is not None:
                        n = ("ot", ot)
                        vacant(pe, n, b, [("pv", ot)])
                        for k in range(KD):
                            ins = nc.tensor.transpose(at(n)[:, k * P:(k + 1) * P],
                                                      o_sb[:, ot % 2, k * P:(k + 1) * P], id_f[:, :])
                        done(ins, n)
                for o in range(KD):
                    n = ("x1t", o)
                    vacant(pe, n, b, [("ot", i) for i in range(TB)] if o == 0 else ())
                    for k in range(KD):
                        ins = mm(at(n)[:, :], wo_sb[:, k, o * P:(o + 1) * P], ot_sb[:, k, :],
                                 start=(k == 0), stop=(k == KD - 1))
                    done(ins, n)
                for t2 in range(TB // 2):
                    n = ("x1", t2)
                    vacant(pe, n, b, [("x1t", o) for o in range(KD)] if t2 == 0 else ())
                    for u in range(2):
                        t = 2 * t2 + u
                        for k in range(KD):
                            ins = nc.tensor.transpose(at(n)[:, u * D + k * P:u * D + (k + 1) * P],
                                                      x1t[:, k, t * P:(t + 1) * P], id_f[:, :])
                    done(ins, n)
                for j in range(KF):
                    n = ("hid", j)
                    vacant(pe, n, b, [("fold_i", n4) for n4 in range(2 * KD)] if j == 0 else ())
                    for k in range(KD):
                        ins = mm(at(n)[:, :], wi_eff[:, k, j * P:(j + 1) * P], x1t[:, k, :],
                                 start=(k == 0), stop=(k == KD - 1))
                    done(ins, n)
                for t2 in range(TB // 2):
                    n = ("h", t2)
                    vacant(pe, n, b, [("fold_o", n4) for n4 in range(KF // 2)] + [("hid", 0)] if t2 == 0 else ())
                    for u in range(2):
                        t = 2 * t2 + u
                        for j in range(KF):
                            if t == 0 and j > 0:
                                drained(pe, ("hid", j), b)
                            ins = mm(at(n)[:, u * D:(u + 1) * D], hid[:, j, t * P:(t + 1) * P], wf_eff[:, j, :],
                                     start=(j == 0), stop=(j == KF - 1))
                    done(ins, n)
                for k in range(KD):
                    n = ("ht", k)
                    vacant(pe, n, b, [("h", t2) for t2 in range(TB // 2)] if k == 0 else ())
                    for t in range(TB):
                        ins = nc.tensor.transpose(at(n)[:, t * P:(t + 1) * P], h_sb[:, t, k * P:(k + 1) * P],
                                                  id_f[:, :])
                    done(ins, n)
                n = ("gate", 0)
                vacant(pe, n, b, [("ht", k) for k in range(KD)])
                for t in range(TB):
                    for k in range(KD):
                        ins = mm(at(n)[:, t * NE:(t + 1) * NE], ht_sb[:, k, t * P:(t + 1) * P], gw_sb[:, k, :],
                                 start=(k == 0), stop=(k == KD - 1))
                done(ins, n)

            pe.wait_ge(s_const, 16 * N_CONST)
            pe.wait_ge(s_idb, 1)
            pe.wait_ge(s_prep, 1)
            with pe.Fori(0, B) as b:
                batch(b)

            pe.wait_ge(s_ohot, 1)
            pe.wait_ge(s_rconst, 16 * N_RC)
            pe.wait_ge(free[PRE_BANK], before_b[PRE_BANK] + 1)
            hots_flat = hots[:, :, :].rearrange("p t e -> p (t e)")
            mm(bank[PRE_BANK][:, 0:NT * NE], tri_sb[:, :], hots_flat, start=True, stop=True
               ).then_inc(full[PRE_BANK], 1)
            pe.wait_ge(free[TOT_BANK], before_b[TOT_BANK] + 1)
            mm(bank[TOT_BANK][:, 0:NT * NE], ones_b[:, :], hots_flat, start=True, stop=True
               ).then_inc(full[TOT_BANK], 1)
            pe.wait_ge(free[ID_BANK], before_b[ID_BANK] + 1)
            n = 0
            for c in range(2):
                for g in range(4):
                    pe.wait_ge(s_hit, 4 * c + g + 1)
                    for t in range(g * NT // 4, (g + 1) * NT // 4):
                        ins = mm(bank[ID_BANK][:, 0:2 * TILES], hit_r[:, t, :],
                                 hit_v[:, t % (NT // 4), :, :].rearrange("p a j -> p (a j)"),
                                 start=(n == 0), stop=(n == 2 * NT - 1))
                        n += 1
                    ins.then_inc(s_hitu, 1)
            pe.wait_ge(s_route, 1)
            pe.wait_ge(s_w1, 16 * NE)

            def expert(j):
                return pe.value_load(etab[0:1, bass.ds(j, 1)], min_val=0, max_val=NE - 1)

            def up(i, j):
                return before_c[i] + 1 + j

            def x_trans(j):
                pe.wait_ge(s_xg, 16 * j + 16)
                pe.wait_ge(free[BX], up(BX, j))
                for k in range(KD):
                    ins = nc.tensor.transpose(bank[BX][:, k * P:(k + 1) * P], xg[:, k * P:(k + 1) * P], id_f[:, :])
                ins.then_inc(full[BX], 1)

            def layer1(j):
                e = expert(j)
                pe.wait_ge(free[BX], up(BX, j) + 1)
                for k in range(KD):
                    ins = mm(bank[BL1][:, :], xgt[:, k, :],
                             w1_sb[:, bass.ds(e, 1), k, :].rearrange("p o n -> p (o n)"),
                             start=(k == 0), stop=(k == KD - 1))
                ins.then_inc(full[BL1], 1)

            def g_trans(j, g, s_g, bt):
                pe.wait_ge(s_g, j + 1)
                pe.wait_ge(free[bt], up(bt, j))
                for k in range(KH):
                    ins = nc.tensor.transpose(bank[bt][:, k * P:(k + 1) * P], g[:, k * P:(k + 1) * P], id_f[:, :])
                ins.then_inc(full[bt], 1)

            def layer2(j, e, half):
                if half == 0:
                    pe.wait_ge(free[BT1], up(BT1, j) + 1)
                for k in range(2 * half, 2 * half + 2):
                    ins = mm(bank[BL2][:, :], g1t[:, k, :],
                             w2_sb[:, bass.ds(e, 1), k, :].rearrange("p o n -> p (o n)"),
                             start=(k == 0), stop=(k == KH - 1))
                if half == 1:
                    ins.then_inc(full[BL2], 1)

            def layer3(j):
                e = expert(j)
                pe.wait_ge(free[BT2], up(BT2, j) + 1)
                pe.wait_ge(free[BL3], up(BL3, j))
                for k in range(KH):
                    ins = mm(bank[BL3][:, 0:D], g2t[:, k, :],
                             w3_sb[:, bass.ds(e, 1), k, :].rearrange("p o n -> p (o n)"),
                             start=(k == 0), stop=(k == KH - 1))
                ins.then_inc(full[BL3], 1)

            def step(j, has):
                if has(2):
                    layer1(j + 2)
                if has(0):
                    g_trans(j, g2, s_g2, BT2)
                if has(1):
                    e = expert(j + 1)
                    layer2(j + 1, e, 0)
                if has(0):
                    layer3(j)
                if has(3):
                    x_trans(j + 3)
                if has(1):
                    layer2(j + 1, e, 1)
                if has(2):
                    g_trans(j + 2, g1, s_g1, BT1)

            for j in (-3, -2):
                step(j, lambda d: 0 <= j + d)
            pe.wait_ge(s_w23, 16 * (2 + 2 * NE))
            step(-1, lambda d: -1 + d >= 0)
            with pe.Fori(0, TILES - 3) as j:
                step(j, lambda d: True)
            for j in range(TILES - 3, TILES):
                step(j, lambda d: j + d < TILES)

        @block.scalar
        def _(act):
            act.wait_ge(s_const, 16 * N_CONST)
            nc.scalar.copy(id_b[:, :], id_f[:, :])
            nc.scalar.copy(mask_b[:, :], mask_f[:, :]).then_inc(s_idb, 1)
            act.sem_inc(s_x1out, 1)

            def batch(b):
                act.wait_ge(s_in, b * 48 + 48)
                for o in range(KD):
                    n = ("cond", o)
                    filled(act, n, b)
                    taken(nc.scalar.activation(cond[:, o, :], at(n)[:, :], ACT.Identity, bias=bc_sb[:, o:o + 1]), n)
                for c in range(HC):
                    filled(act, ("q", c), b)
                    if c > 0:
                        drained(act, ("q", c - 1), b)
                    nc.scalar.copy(q_hi[:, :], at(("q", c))[:, :]).then_inc(s_hi, 1)
                    filled(act, ("k", c), b)
                    nc.scalar.copy(kh_sb[:, c, :], at(("k", c))[:, :]).then_inc(s_hi, 1)
                for t2 in range(TB // 2):
                    n = ("v", t2)
                    filled(act, n, b)
                    taken(nc.scalar.copy(v_sb[:, 2 * t2:2 * t2 + 2, :].rearrange("p t d -> p (t d)"), at(n)[:, :]), n)
                for step in range(UNITS + OT_LAG):
                    s, t, pv, ot = units_at(step)
                    if s is not None:
                        i, h = divmod(s, HEADS)
                        n = ("s", s)
                        act.wait_ge(s_max, b * UNITS + (s + 1))
                        if h == 0 and i >= 2:
                            drained(act, ("pv", i - 2), b)
                        taken(nc.scalar.activation(probs[:, s % 4, 0:(i + 1) * P], at(n)[:, 0:(i + 1) * P], ACT.Exp,
                                                   bias=nmax[:, s % 8:s % 8 + 1], accum_out=rsum[:, i % 2, h:h + 1]), n)
                    if t is not None and t % 3 == 2:
                        n = ("t", t)
                        w = (t // HEADS + 1) * P
                        filled(act, n, b)
                        taken(nc.scalar.copy(probs_t[:, t % 4, 0:w], at(n)[:, 0:w]), n)
                    if ot is not None:
                        n = ("ot", ot)
                        filled(act, n, b)
                        taken(nc.scalar.copy(ot_sb[:, :, ot * P:(ot + 1) * P],
                                             at(n)[:, 0:D].rearrange("p (k t) -> p k t", k=KD)), n)
                act.wait_ge(s_x1out, b * 16 + 1)
                for t2 in range(TB // 2):
                    n = ("x1", t2)
                    filled(act, n, b)
                    taken(nc.scalar.copy(x1_sb[:, 2 * t2:2 * t2 + 2, :].rearrange("p t d -> p (t d)"), at(n)[:, :]), n)
                for j in range(0, KF, 2):
                    n = ("hid", j)
                    filled(act, n, b)
                    taken(nc.scalar.activation(hid[:, j, :], at(n)[:, :], ACT.Relu), n)
                n = ("ht", 1)
                filled(act, n, b)
                taken(nc.scalar.copy(ht_sb[:, 1, :], at(n)[:, :]), n)
                act.wait_ge(s_gneg, b + 1)
                nc.scalar.activation(gexp[:, :, :], gexp[:, :, :], ACT.Exp).then_inc(s_gexp, 1)

            with act.Fori(0, B) as b:
                batch(b)

            def gelu(j, z, g, s_z, s_g):
                act.wait_ge(s_z, j + 1)
                nc.scalar.activation(g[:, :], z[:, :], ACT.Gelu).then_inc(s_g, 1)

            def step(j, has):
                if has(2):
                    gelu(j + 2, z1, g1, s_z1, s_g1)
                if has(1):
                    gelu(j + 1, z2, g2, s_z2, s_g2)

            for j in (-2, -1):
                step(j, lambda d: 0 <= j + d)
            with act.Fori(0, TILES - 2) as j:
                step(j, lambda d: True)
            for j in range(TILES - 2, TILES):
                step(j, lambda d: j + d < TILES)

        @block.vector
        def _(dve):
            V = nc.vector
            dve.wait_ge(s_const, 16 * N_CONST)
            V.tensor_scalar(wq_raw[:, :, :].rearrange("p k n -> p (k n)"), wq_raw[:, :, :].rearrange("p k n -> p (k n)"),
                            DH ** -0.5, None, ALU.mult).then_inc(s_prep, 1)
            dve.sem_inc(s_hout, 1)
            dve.wait_ge(s_mid, 32)

            def fold(name, eff, base, b):
                filled(dve, name, b)
                taken(V.scalar_tensor_tensor(eff, at(name)[:, :], 2.0, base, ALU.mult, ALU.add), name)

            def batch(b):
                for n4 in range(2 * KD):
                    k, fh = n4 // 2, n4 % 2
                    fold(("fold_i", n4), wi_eff[:, k, fh * 512:(fh + 1) * 512],
                         wi_base[:, k, fh * 512:(fh + 1) * 512], b)
                for c in range(HC):
                    dve.wait_ge(s_hi, b * (2 * HC) + (2 * c + 1))
                    n = ("q", c)
                    filled(dve, n, b)
                    taken(V.scalar_tensor_tensor(q_sb[:, c, :], q_hi[:, :].bitcast(F32), low_sb[:, 0:1], at(n)[:, :],
                                                 ALU.mult, ALU.add), n)
                    dve.wait_ge(s_hi, b * (2 * HC) + (2 * c + 2))
                    n = ("k", c)
                    filled(dve, n, b)
                    taken(V.scalar_tensor_tensor(kl_sb[:, c, :], kh_sb[:, c, :].bitcast(F32), -1.0, at(n)[:, :],
                                                 ALU.mult, ALU.add), n)
                for n4 in range(KF // 2):
                    fold(("fold_o", n4), wf_eff[:, 2 * n4:2 * n4 + 2, :].rearrange("p j d -> p (j d)"),
                         wf_base[:, 2 * n4:2 * n4 + 2, :].rearrange("p j d -> p (j d)"), b)
                for step in range(UNITS + OT_LAG):
                    s, t, pv, ot = units_at(step)
                    if s is not None:
                        n = ("s", s)
                        i = s // HEADS
                        filled(dve, n, b)
                        V.tensor_reduce(nmax[:, s % 8:s % 8 + 1], at(n)[:, 0:(i + 1) * P], AX.X, ALU.max,
                                        negate=True).then_inc(s_max, 1)
                    if t is not None and t % 3 != 2:
                        n = ("t", t)
                        w = (t // HEADS + 1) * P
                        filled(dve, n, b)
                        taken(V.tensor_copy(probs_t[:, t % 4, 0:w], at(n)[:, 0:w]), n)
                    if pv is not None and pv % HEADS == HEADS - 1:
                        i = pv // HEADS
                        n = ("pv", i)
                        filled(dve, n, b)
                        V.reciprocal(rinv[:, :], rsum[:, i % 2, :]).then_inc(s_chain, 1)
                        dve.wait_ge(s_chain, b * CHAIN + (i + 1))
                        taken(V.tensor_tensor(o_sb[:, i % 2, :].rearrange("p (h d) -> p h d", d=DH),
                                              at(n)[:, 0:D].rearrange("p (h d) -> p h d", d=DH),
                                              rinv[:, :].unsqueeze(2).to_broadcast([P, HEADS, DH]), ALU.mult), n)
                dve.wait_ge(s_xres, b * 16 + 16)
                for o in range(KD):
                    n = ("x1t", o)
                    filled(dve, n, b)
                    taken(V.tensor_tensor(x1t[:, o, :], at(n)[:, :], x_res[:, o, :], ALU.add), n)
                for j in range(1, KF, 2):
                    n = ("hid", j)
                    filled(dve, n, b)
                    taken(V.tensor_scalar(hid[:, j, :], at(n)[:, :], 0.0, None, ALU.max), n)
                dve.wait_ge(s_hout, b * 16 + 1)
                for t2 in range(TB // 2):
                    n = ("h", t2)
                    filled(dve, n, b)
                    taken(V.tensor_copy(h_sb[:, 2 * t2:2 * t2 + 2, 0:D],
                                        at(n)[:, :].rearrange("p (t d) -> p t d", d=D)), n)
                n = ("ht", 0)
                filled(dve, n, b)
                taken(V.tensor_copy(ht_sb[:, 0, :], at(n)[:, :]), n)
                n = ("gate", 0)
                filled(dve, n, b)
                taken(V.tensor_tensor(glog[:, :, :], at(n)[:, 0:TB * NE].rearrange("p (t e) -> p t e", e=NE),
                                      gb_sb[:, :].unsqueeze(1).to_broadcast([P, TB, NE]), ALU.add), n)
                drained(dve, n, b)
                V.tensor_copy(logits[:, bass.ds(b * TB, TB), :], glog[:, :, :])
                V.tensor_reduce(gmax[:, :], glog[:, :, :], AX.X, ALU.max).then_inc(s_chain, 1)
                dve.wait_ge(s_chain, b * CHAIN + (TB + 1))
                V.tensor_tensor(gexp[:, :, :], glog[:, :, :], gmax[:, :].unsqueeze(2).to_broadcast([P, TB, NE]),
                                ALU.subtract).then_inc(s_gneg, 1)
                dve.wait_ge(s_gexp, b + 1)
                V.tensor_reduce(gsum[:, :], gexp[:, :, :], AX.X, ALU.add).then_inc(s_gchain, 1)
                dve.wait_ge(s_gchain, 2 * b + 1)
                V.reciprocal(ginv[:, :], gsum[:, :]).then_inc(s_gchain, 1)
                dve.wait_ge(s_gchain, 2 * b + 2)
                V.tensor_tensor(h_sb[:, :, D:ROW], gexp[:, :, :], ginv[:, :].unsqueeze(2).to_broadcast([P, TB, NE]),
                                ALU.mult).then_inc(s_hdone, 1)

            with dve.Fori(0, B) as b:
                batch(b)

            links = [0]

            def link(ins):
                links[0] += 1
                ins.then_inc(s_rchain, 1)
                dve.wait_ge(s_rchain, links[0])

            def over_e(ap):
                return ap.unsqueeze(2).to_broadcast([P, NT, NE])

            dve.wait_ge(s_hout, 16 * B + 1)
            dve.wait_ge(s_x1out, 16 * B + 1)
            for i in range(8):
                dve.wait_ge(full[i], before_b[i])
                dve.wait_ge(free[i], before_b[i] + 1)
            dve.wait_ge(s_rconst, 16 * N_RC)
            link(V.memset(ones_b[:, :], 1.0))
            link(V.tensor_copy(tri_sb[:, :], tri_f[:, :]))
            for c in range(2):
                src = logits if c == 0 else lg2
                link(V.tensor_reduce(m1[:, :], src[:, :, :], AX.X, ALU.max))
                link(V.tensor_tensor(rk[:, :, :], src[:, :, :], over_e(m1[:, :]), ALU.is_equal))
                link(V.tensor_tensor(rk[:, :, :], rk[:, :, :],
                                     iota_t_sb[:, 1:NE + 1].unsqueeze(1).to_broadcast([P, NT, NE]), ALU.mult))
                link(V.tensor_scalar(run[0][:, :, :], rk[:, :, :], 0.0, 1000.0, ALU.is_equal, ALU.mult))
                link(V.tensor_tensor(rk[:, :, :], rk[:, :, :], run[0][:, :, :], ALU.add))
                link(V.tensor_reduce(m1[:, :], rk[:, :, :], AX.X, ALU.min))
                link(V.tensor_tensor(hot[c][:, :, :], rk[:, :, :], over_e(m1[:, :]), ALU.is_equal))
                if c == 0:
                    link(V.scalar_tensor_tensor(lg2[:, :, :].rearrange("p t e -> p (t e)"),
                                                hot[0][:, :, :].rearrange("p t e -> p (t e)"), -BIG,
                                                logits[:, :, :].rearrange("p t e -> p (t e)"), ALU.mult, ALU.add))
            V.tensor_tensor(hots[:, :, :], hot[0][:, :, :], hot[1][:, :, :], ALU.add).then_inc(s_ohot, 1)
            dve.wait_ge(full[TOT_BANK], before_b[TOT_BANK] + 1)
            link(V.tensor_copy(run[0][:, :, :].rearrange("p t e -> p (t e)"), bank[TOT_BANK][:, 0:NT * NE]))
            cur = 0
            for sh in (1, 2, 4, 8, 16):
                link(V.tensor_copy(run[1 - cur][:, 0:sh, :], run[cur][:, 0:sh, :]))
                link(V.tensor_tensor(run[1 - cur][:, sh:NT, :], run[cur][:, sh:NT, :], run[cur][:, 0:NT - sh, :], ALU.add))
                cur = 1 - cur
            link(V.tensor_copy(cnt[:, :], run[cur][:, NT - 1, :]))
            link(V.tensor_tensor(run[1 - cur][:, :, :].rearrange("p t e -> p (t e)"),
                                 run[cur][:, :, :].rearrange("p t e -> p (t e)"), bank[TOT_BANK][:, 0:NT * NE],
                                 ALU.subtract))
            dve.sem_inc(free[TOT_BANK], 1)
            dve.wait_ge(full[PRE_BANK], before_b[PRE_BANK] + 1)
            V.tensor_tensor(pre[:, :, :].rearrange("p t e -> p (t e)"),
                            run[1 - cur][:, :, :].rearrange("p t e -> p (t e)"), bank[PRE_BANK][:, 0:NT * NE],
                            ALU.add).then_inc(free[PRE_BANK], 1)
            dve.wait_ge(free[PRE_BANK], before_b[PRE_BANK] + 2)
            link(V.tensor_tensor(cmpt[:, :, :], cnt[:, :].unsqueeze(2).to_broadcast([P, NE, 2 * NT]),
                                 thr_sb[:, :].unsqueeze(1).to_broadcast([P, NE, 2 * NT]), ALU.is_gt))
            link(V.tensor_reduce(ntile[:, :], cmpt[:, :, :], AX.X, ALU.add))
            link(V.memset(tbase[:, :], 0.0))
            for e in range(NE):
                link(V.tensor_tensor(tbase[:, e + 1:e + 2], tbase[:, e:e + 1], ntile[:, e:e + 1], ALU.add))
            link(V.memset(eacc[0][:, :], 0.0))
            ecur = 0
            for e in range(1, NE):
                link(V.scalar_tensor_tensor(eacc[1 - ecur][:, :], iota_t_sb[0:1, 0:TILES], tbase[0:1, e:e + 1],
                                            eacc[ecur][:, :], ALU.is_ge, ALU.add))
                ecur = 1 - ecur
            link(V.tensor_copy(etab[:, :], eacc[ecur][:, :]))
            link(V.scalar_tensor_tensor(pre[:, :, :], tbase[:, 0:NE].unsqueeze(1).to_broadcast([P, NT, NE]), float(P),
                                        pre[:, :, :], ALU.mult, ALU.add))
            n_hit = 0
            for c in range(2):
                link(V.tensor_tensor(rk[:, :, :], hot[c][:, :, :], pre[:, :, :], ALU.mult))
                link(V.tensor_reduce(slot[:, :], rk[:, :, :], AX.X, ALU.add))
                link(V.tensor_copy(s_i[:, 0, :], slot[:, :]))
                link(V.tensor_scalar(s_i[:, 1, :], s_i[:, 0, :], 7, None, ALU.arith_shift_right))
                link(V.tensor_copy(s_j[:, c, :], s_i[:, 1, :]))
                link(V.scalar_tensor_tensor(s_r[:, c, :], s_j[:, c, :], -float(P), slot[:, :], ALU.mult, ALU.add))
                if c == 1:
                    dve.wait_ge(s_hitu, 4)
                link(V.tensor_tensor(hit_r[:, :, :], iota_r_sb[:, :].unsqueeze(1).to_broadcast([P, NT, P]),
                                     s_r[:, c, :].unsqueeze(2).to_broadcast([P, NT, P]), ALU.is_equal))
                for g in range(4):
                    q = NT // 4
                    ts_ = slice(g * q, (g + 1) * q)
                    if n_hit > 0:
                        dve.wait_ge(s_hitu, n_hit)
                    link(V.tensor_tensor(hit_j[:, :, :], iota_t_sb[:, 0:TILES].unsqueeze(1).to_broadcast([P, q, TILES]),
                                         s_j[:, c, ts_].unsqueeze(2).to_broadcast([P, q, TILES]), ALU.is_equal))
                    for a in range(2):
                        ins = V.tensor_tensor(hit_v[:, :, a, :], hit_j[:, :, :],
                                              tok_sb[:, ts_, a].unsqueeze(2).to_broadcast([P, q, TILES]), ALU.mult)
                        if a == 0:
                            link(ins)
                        else:
                            ins.then_inc(s_hit, 1)
                            dve.wait_ge(s_hit, n_hit + 1)
                    n_hit += 1
            dve.wait_ge(s_hitu, 8)
            link(V.tensor_copy(ids_f[:, :], bank[ID_BANK][:, 0:TILES]))
            V.tensor_tensor(ids_g[:, :], ids_f[:, :], bank[ID_BANK][:, TILES:2 * TILES], ALU.add
                            ).then_inc(free[ID_BANK], 1)
            dve.wait_ge(free[ID_BANK], before_b[ID_BANK] + 2)
            link(V.tensor_scalar(ids_f[:, :], ids_g[:, :], -1.0, 0.0, ALU.add, ALU.max))
            link(V.tensor_copy(gather_id[:, :], ids_f[:, :]))
            link(V.tensor_scalar(ids_f[:, :], ids_g[:, :], 0.0, float(2 * B * S), ALU.is_equal, ALU.mult))
            link(V.scalar_tensor_tensor(ids_f[:, :], ids_g[:, :], -1.0, ids_f[:, :], ALU.add, ALU.add))
            V.tensor_copy(scatter_id[:, :], ids_f[:, :]).then_inc(s_route, 1)
            dve.wait_ge(s_route, 1)
            dve.wait_ge(s_w23, 16 * (2 + 2 * NE))

            def expert(j):
                return dve.value_load(etab[0:1, bass.ds(j, 1)], min_val=0, max_val=NE - 1)

            def up(i, j):
                return before_c[i] + 1 + j

            def fl(i, j):
                return before_b[i] + (1 if i < 2 else 0) + 1 + j

            def x_evac(j):
                e = expert(j)
                dve.wait_ge(s_xg, 16 * j + 16)
                V.tensor_copy(wsel[:, bass.ds(j, 1)], xg[:, bass.ds(e + D, 1)]).then_inc(s_wsel, 1)
                dve.wait_ge(full[BX], fl(BX, j))
                V.tensor_copy(xgt[:, :, :].rearrange("p k t -> p (k t)"), bank[BX][:, 0:D]).then_inc(free[BX], 1)

            def add_bias(j, bl, z, bias, s_z):
                e = expert(j)
                dve.wait_ge(full[bl], fl(bl, j))
                V.tensor_tensor(z[:, :], bank[bl][:, :], bias[:, bass.ds(e, 1), :].rearrange("p o n -> p (o n)"),
                                ALU.add).then_inc(s_z, 1)

            def t_evac(j, bt, gt):
                dve.wait_ge(full[bt], fl(bt, j))
                V.tensor_copy(gt[:, :, :].rearrange("p k t -> p (k t)"), bank[bt][:, :]).then_inc(free[bt], 1)

            def first(d):
                return True

            def step(j, has):
                if has(2):
                    add_bias(j + 2, BL1, z1, b1_sb, s_z1)
                if has(0):
                    t_evac(j, BT2, g2t)
                    e = expert(j)
                    dve.wait_ge(full[BL3], fl(BL3, j))
                    V.tensor_tensor(y0[:, :], bank[BL3][:, 0:D], b3_sb[:, bass.ds(e, 1), :].rearrange("p o n -> p (o n)"),
                                    ALU.add).then_inc(free[BL3], 1)
                    dve.wait_ge(free[BL3], up(BL3, j) + 1)
                    if has is not first:
                        dve.wait_ge(s_add, 16 * j)
                    V.tensor_scalar(y_sb[:, :], y0[:, :], wsel[:, bass.ds(j, 1)], None, ALU.mult).then_inc(s_y, 1)
                if has(3):
                    x_evac(j + 3)
                if has(1):
                    add_bias(j + 1, BL2, z2, b2_sb, s_z2)
                if has(2):
                    t_evac(j + 2, BT1, g1t)

            for j in (-3, -2, -1):
                step(j, lambda d: 0 <= j + d)
            step(0, first)
            with dve.Fori(1, TILES - 3) as j:
                step(j, lambda d: True)
            for j in range(TILES - 3, TILES):
                step(j, lambda d: j + d < TILES)

        @block.gpsimd
        def _(pool):
            pool.wait_ge(s_route, 1)
            pool.wait_ge(s_hout, 16 * B + 1)
            pool.wait_ge(s_x1out, 16 * B + 1)

            def gather(j, vj1):
                nc.gpsimd.tensor_copy(gid[:, :], gather_id[:, bass.ds(j, 1)]).then_inc(s_gid, 1)
                pool.wait_ge(s_gid, vj1)
                pool.sem_inc(s_tick, 1)
                nc.gpsimd.indirect_dma_start(
                    xg[:, :], None, hrows, bass.IndirectOffsetOnAxis(ap=gid[:, 0:1], axis=0),
                    bounds_check=B * S - 1, oob_is_err=False).then_inc(s_xg, 16)

            def scatter(j, vj1):
                nc.gpsimd.tensor_copy(sid[:, :], scatter_id[:, bass.ds(j, 1)]).then_inc(s_sid, 1)
                pool.wait_ge(s_sid, vj1)
                pool.wait_ge(s_y, vj1)
                pool.sem_inc(s_tick, 1)
                nc.gpsimd.indirect_dma_start(
                    out_rows, bass.IndirectOffsetOnAxis(ap=sid[:, 0:1], axis=0), y_sb[:, :], None,
                    bounds_check=B * S - 1, oob_is_err=False, compute_op=ALU.add).then_inc(s_add, 16)

            def xg_free(v_bank, v_sel):
                pool.wait_ge(full[BX], v_bank)
                pool.sem_inc(s_tick, 1)
                pool.wait_ge(s_wsel, v_sel)
                pool.sem_inc(s_tick, 1)

            filled_x = before_b[BX] + b_uses[BX]
            gather(0, 1)
            for j in range(3):
                xg_free(filled_x + j + 1, j + 1)
                gather(j + 1, j + 2)
            scatter(0, 1)
            xg_free(filled_x + 4, 4)
            gather(4, 5)
            with pool.Fori(1, TILES - 4) as j:
                v_added, v_j1, v_j4, v_j5 = (pool.snap(v) for v in (16 * j, j + 1, j + 4, j + 5))
                v_bx = pool.snap(j + (filled_x + 4))
                pool.wait_ge(s_add, v_added)
                scatter(j, v_j1)
                xg_free(v_bx, v_j4)
                gather(v_j4, v_j5)
            for j in range(TILES - 4, TILES):
                pool.wait_ge(s_add, 16 * j)
                scatter(j, j + 1)


_OUTS = [((B, S, D), "float32")]


def kernel(**inputs):
    import numpy as _np
    import concourse.bacc as _bacc
    from concourse import mybir as _mybir
    from concourse.bass_utils import run_bass_kernel_spmd as _run

    def chunked(w):
        n, k, m = w.shape
        return w.reshape(n, k // P, P, m).transpose(0, 2, 1, 3)

    def get(name):
        return _np.asarray(inputs[name])

    def strips(w):
        w = w.reshape(D, HEADS, DH)
        return chunked(_np.concatenate([w, w], axis=2).reshape(1, D, HEADS * 2 * DH))[0]

    def lora_rows(wi_a, wi_b, wo_a, wo_b):
        return _np.concatenate([wi_a, wi_b.swapaxes(-1, -2), wo_a, wo_b.swapaxes(-1, -2)], axis=-1)

    iota = _np.arange(P, dtype=_np.float32)
    tokens = (_np.arange(NT)[None, :] * P + _np.arange(P)[:, None] + 1)
    data = {
        "xT": chunked(get("x").transpose(0, 2, 1)),
        "cond_w": chunked(get("L0_cond_weight").transpose(0, 2, 1)),
        "cond_b": get("L0_cond_bias").reshape(NE, KD, P).transpose(0, 2, 1),
        "itok": get("itok_B_0_7").reshape(1, B),
        "wq": strips(get("L0_attn_W_Q")),
        "wk": strips(get("L0_attn_W_K")),
        "wv": chunked(get("L0_attn_W_V")[None])[0],
        "wo": chunked(get("L0_attn_W_o")[None])[0],
        "wi_t": chunked(get("L0_cond2_wi").T[None])[0],
        "wo_t": chunked(get("L0_cond2_wo").T[None])[0],
        "lora_c": lora_rows(*(get("L0_cond2_common_" + n) for n in ("wi_a", "wi_b", "wo_a", "wo_b"))),
        "lora_e": lora_rows(*(get("L0_cond2_experts_" + n) for n in ("wi_a", "wi_b", "wo_a", "wo_b"))),
        "gate_w": chunked(get("L0_ffn_gate_w")[None])[0],
        "gate_b": get("L0_ffn_gate_b").reshape(NE),
        "w1": chunked(get("L0_ffn_w1")),
        "w2": chunked(get("L0_ffn_w2")),
        "w3": chunked(get("L0_ffn_w3")),
        "b1": get("L0_ffn_b1").reshape(NE * H),
        "b2": get("L0_ffn_b2").reshape(NE * H),
        "b3": get("L0_ffn_b3").reshape(NE * D),
        "ident": _np.eye(P, dtype=_np.float32),
        "maskd": _np.triu(_np.full((P, P), -BIG, _np.float32), 1),
        "tri": _np.triu(_np.ones((P, P), _np.float32), 1),
        "low": -((_np.arange(P) % STRIP) >= DH).astype(_np.float32).reshape(P, 1),
        "iota_r": _np.tile(iota, (P, 1)),
        "iota_t": _np.tile(_np.arange(TILES, dtype=_np.float32), (P, 1)),
        "tok": _np.stack([tokens % 64, tokens - tokens % 64], axis=2).astype(_np.float32),
        "thr": _np.tile(_np.arange(2 * NT, dtype=_np.float32) * P, (P, 1)),
    }
    nc = _bacc.Bacc("TRN2", target_bir_lowering=False, num_devices=1)
    arrays, args = {}, []
    for name, a in data.items():
        a = _np.ascontiguousarray(a)
        arrays[f"in_{name}"] = a
        args.append(nc.dram_tensor(f"in_{name}", a.shape, _mybir.dt.from_np(a.dtype), kind="ExternalInput").ap())
    for i, (shape, dtype) in enumerate(_OUTS):
        dt = _mybir.dt.from_np(_np.dtype(dtype))
        args.append(nc.dram_tensor(f"out_{i}", shape, dt, kind="ExternalOutput").ap())
    build_kernel(nc, *args)
    r = _run(nc, [arrays], core_ids=[0])
    return r.results[0]["out_0"]
```

```python
from contextlib import ExitStack

import concourse.bass as bass
from concourse import mybir

F32 = mybir.dt.float32
F32R = mybir.dt.float32r
BF16 = mybir.dt.bfloat16
I32 = mybir.dt.int32
U32 = mybir.dt.uint32
ALU = mybir.AluOpType
ACT = mybir.ActivationFunctionType
AX = mybir.AxisListType

P = 128
B, S, D = 8, 512, 256
KD = D // P
TB = S // P
HEADS, DH = 16, 16
STRIP = 32
HC = HEADS * STRIP // P
F = 1024
KF = F // P
R = 16
LORA = D + F + F + D
NE = 8
H = 512
KH = H // P
NT = B * TB
ROW = D + NE
AHEAD = 4
TILES = (2 * B * S + NE * (P - 1)) // P
BIG = 1.0e30
UNITS = TB * HEADS
PAIR = 2
T_LAG, PV_LAG = 1, 2
INV_LAG, RT_LAG, NORM_LAG = 1, 2, 3
STEPS = UNITS // PAIR + NORM_LAG


def units_at(step):
    def units(n):
        return range(PAIR * n, PAIR * n + PAIR) if 0 <= PAIR * n < UNITS else ()

    def tile(n):
        per = HEADS // PAIR
        return n // per if 0 <= n < UNITS // PAIR and n % per == per - 1 else None
    return (units(step), units(step - T_LAG), units(step - PV_LAG),
            tile(step - INV_LAG), tile(step - RT_LAG), tile(step - NORM_LAG))


def psum_plan():
    ring, tring = [0, 1, 2, 3], [4, 5]
    uses = [0] * 8
    turn = {"ring": 0, "tring": 0}
    plan = {}

    def take(name, kind):
        banks = ring if kind == "ring" else tring
        bank = banks[turn[kind] % len(banks)]
        turn[kind] += 1
        plan[name] = (bank, uses[bank])
        uses[bank] += 1

    for o in range(KD):
        take(("cond", o), "ring")
    for c in range(HC):
        take(("q", c), "ring")
        take(("k", c), "ring")
    for t in range(TB // 2):
        take(("v", t), "ring")
    for step in range(STEPS):
        ss, ts, pvs, _, rt, _ = units_at(step)
        for s in ss:
            take(("s", s), "ring")
        for pv in pvs:
            if pv % HEADS == 0:
                bank = 6 + (pv // HEADS) % 2
                plan[("pv", pv // HEADS)] = (bank, uses[bank])
                uses[bank] += 1
        for t in ts:
            take(("t", t), "tring")
        if rt is not None:
            take(("rt", rt), "tring")
    for n in range(2 * KD):
        take(("fold_i", n), "ring")
    for o in range(KD):
        take(("x1t", o), "ring")
    for n in range(KF // 2):
        take(("fold_o", n), "ring")
    for j in range(KF):
        take(("hid", j), "ring")
    for t in range(TB // 2):
        take(("x1", t), "ring")
    for t in range(TB // 2):
        take(("h", t), "ring")
    for k in range(KD):
        take(("ht", k), "ring")
    take(("gate", 0), "ring")
    return plan, uses


def build_kernel(nc, xT, x_cond_w, x_cond_b, itok, wq, wk, wv, wo, wi_t, wo_t, lora_c, lora_e,
                 gate_w, gate_b, w1, w2, w3, b1, b2, b3, ident, maskd, tri, low, iota_r, iota_t,
                 tok, thr, out):
    plan, uses = psum_plan()
    hrows = nc.dram_tensor("hrows", [B * S, ROW], F32, kind="Internal").ap()
    out_rows = out.rearrange("b s d -> (b s) d")

    outer = ExitStack()
    part_a = ExitStack()
    with outer:
        def sb(name, shape, dt, ctx=outer):
            return ctx.enter_context(nc.sbuf_tensor(name, shape, dt))

        def sem(name):
            return outer.enter_context(nc.semaphore(name))

        bank = [outer.enter_context(nc.psum_tensor(f"bank{i}", [P, 512], F32)) for i in range(8)]

        id_f = sb("id_f", [P, P], F32)
        id_b = sb("id_b", [P, P], BF16)
        mask_b = sb("mask_b", [P, P], BF16)
        mask_f = sb("mask_f", [P, P], F32)
        itok_sb = sb("itok_sb", [1, B], I32)
        low_sb = sb("low_sb", [P, 1], F32)
        gb_sb = sb("gb_sb", [P, NE], F32)
        logits = sb("logits", [P, NT, NE], F32)
        w1_sb = sb("w1_sb", [P, NE, KD, H], F32)
        b3_sb = sb("b3_sb", [P, NE, D], F32)

        x_in = sb("x_in", [P, KD, S], F32, part_a)
        x_res = sb("x_res", [P, KD, S], F32, part_a)
        wc_sb = sb("wc_sb", [P, KD, D], F32, part_a)
        bc_sb = sb("bc_sb", [P, KD], F32, part_a)
        cond = sb("cond", [P, KD, S], F32, part_a)
        wq_raw = sb("wq_raw", [P, KD, HC * P], F32, part_a)
        wk_sb = sb("wk_sb", [P, KD, HC * P], F32, part_a)
        wv_sb = sb("wv_sb", [P, KD, D], F32, part_a)
        wo_sb = sb("wo_sb", [P, KD, D], F32, part_a)
        q_sb = sb("q_sb", [P, HC, S], F32R, part_a)
        kh_sb = sb("kh_sb", [P, HC, S], F32R, part_a)
        kl_sb = sb("kl_sb", [P, HC, S], F32R, part_a)
        q_hi = sb("q_hi", [P, S], F32R, part_a)
        v_sb = sb("v_sb", [P, TB, HEADS // 2, 2, 2, DH], F32, part_a)
        probs = sb("probs", [P, 4, S], F32, part_a)
        probs_t = sb("probs_t", [P, 4, S], F32, part_a)
        nmax = sb("nmax", [P, 8], F32, part_a)
        rsum = sb("rsum", [P, 2, HEADS], F32, part_a)
        rinv = sb("rinv", [P, HEADS], F32, part_a)
        rrep = sb("rrep", [P, D], F32, part_a)
        rt_sb = sb("rt_sb", [P, D], F32, part_a)
        ot_sb = sb("ot_sb", [P, KD, S], F32, part_a)
        x1t = sb("x1t", [P, KD, S], F32, part_a)
        x1_sb = sb("x1_sb", [P, TB, D], F32, part_a)
        wi_base = sb("wi_base", [P, KD, F], F32, part_a)
        wi_eff = sb("wi_eff", [P, KD, F], F32, part_a)
        wf_base = sb("wf_base", [P, KF, D], F32, part_a)
        wf_eff = sb("wf_eff", [P, KF, D], F32, part_a)
        lora = sb("lora", [2 * R, LORA], F32, part_a)
        hid = sb("hid", [P, KF, S], F32, part_a)
        h_sb = sb("h_sb", [P, TB, ROW], F32, part_a)
        ht_sb = sb("ht_sb", [P, KD, S], F32, part_a)
        gw_sb = sb("gw_sb", [P, KD, NE], F32, part_a)
        glog = sb("glog", [P, TB, NE], F32, part_a)
        gmax = sb("gmax", [P, TB], F32, part_a)
        gexp = sb("gexp", [P, TB, NE], F32, part_a)
        gsum = sb("gsum", [P, TB], F32, part_a)
        ginv = sb("ginv", [P, TB], F32, part_a)
        part_a.close()

        w2_sb = sb("w2_sb", [P, NE, KH, H], F32)
        w3_sb = sb("w3_sb", [P, NE, KH, D], F32)
        b1_sb = sb("b1_sb", [P, NE, H], F32)
        b2_sb = sb("b2_sb", [P, NE, H], F32)
        route = ExitStack()
        etab = sb("etab", [1, TILES, AHEAD], I32)
        gather_id = sb("gather_id", [P, TILES], U32)
        scatter_id = sb("scatter_id", [P, TILES], U32)
        with route:
            tri_f = sb("tri_f", [P, P], F32, route)
            tri_sb = sb("tri_sb", [P, P], BF16, route)
            ones_b = sb("ones_b", [P, P], BF16, route)
            iota_r_sb = sb("iota_r_sb", [P, P], F32, route)
            iota_t_sb = sb("iota_t_sb", [P, TILES], F32, route)
            tok_sb = sb("tok_sb", [P, NT, 2], F32, route)
            thr_sb = sb("thr_sb", [P, NT * 2], F32, route)
            m1 = sb("m1", [P, NT], F32, route)
            rk = sb("rk", [P, NT, NE], F32, route)
            lg2 = sb("lg2", [P, NT, NE], F32, route)
            hot = [sb(f"hot{c}", [P, NT, NE], F32, route) for c in range(2)]
            hots = sb("hots", [P, NT, NE], BF16, route)
            run = [sb(f"run{c}", [P, NT, NE], F32, route) for c in range(2)]
            pre = sb("pre", [P, NT, NE], F32, route)
            cnt = sb("cnt", [P, NE], F32, route)
            cmpt = sb("cmpt", [P, NE, NT * 2], F32, route)
            ntile = sb("ntile", [P, NE], F32, route)
            tbase = sb("tbase", [P, NE + 1], F32, route)
            slot = sb("slot", [P, NT], F32, route)
            s_r = sb("s_r", [P, 2, NT], F32, route)
            s_j = sb("s_j", [P, 2, NT], F32, route)
            s_i = sb("s_i", [P, 2, NT], I32, route)
            hit_r = sb("hit_r", [P, NT, P], BF16, route)
            hit_j = sb("hit_j", [P, NT // 4, TILES], F32, route)
            hit_v = sb("hit_v", [P, NT // 4, 2, TILES], BF16, route)
            ids_f = sb("ids_f", [P, TILES], F32, route)
            ids_g = sb("ids_g", [P, TILES], F32, route)
            etab_f = sb("etab_f", [1, TILES], F32, route)
            eacc = [sb(f"eacc{c}", [1, TILES], F32, route) for c in range(2)]
        xg = sb("xg", [P, ROW], F32)
        xgt = sb("xgt", [P, KD, P], F32)
        gid = sb("gid", [P, 1], U32)
        sid = sb("sid", [P, 1], U32)
        wsel = sb("wsel", [P, TILES], F32)
        z1 = sb("z1", [P, H], F32)
        z2 = sb("z2", [P, H], F32)
        g1 = sb("g1", [P, H], F32)
        g2 = sb("g2", [P, H], F32)
        g1t = sb("g1t", [P, KH, P], F32)
        g2t = sb("g2t", [P, KH, P], F32)
        y0 = sb("y0", [P, D], F32)
        y_sb = sb("y_sb", [P, D], F32)

        full = [sem(f"bank{i}_filled") for i in range(8)]
        free = [sem(f"bank{i}_drained") for i in range(8)]
        s_const = sem("s_const")
        s_mid = sem("s_mid")
        s_in = sem("s_in")
        s_xres = sem("s_xres")
        s_lora = sem("s_lora")
        s_x1out = sem("s_x1out")
        s_hout = sem("s_hout")
        s_prep = sem("s_prep")
        s_idb = sem("s_idb")
        s_hi = sem("s_hi")
        s_max = sem("s_max")
        s_chain = sem("s_chain")
        s_rrep = sem("s_rrep")
        s_vzero = sem("s_vzero")
        s_gneg = sem("s_gneg")
        s_gexp = sem("s_gexp")
        s_gchain = sem("s_gchain")
        s_hdone = sem("s_hdone")
        s_rchain = sem("s_rchain")
        s_rconst = sem("s_rconst")
        s_ohot = sem("s_ohot")
        s_cnts = sem("s_cnts")
        s_hit = sem("s_hit")
        s_hitu = sem("s_hitu")
        s_route = sem("s_route")
        s_w23 = sem("s_w23")
        s_w1 = sem("s_w1")
        s_gid = sem("s_gid")
        s_xg = sem("s_xg")
        s_wsel = sem("s_wsel")
        s_z1 = sem("s_z1")
        s_g1 = sem("s_g1")
        s_z2 = sem("s_z2")
        s_g2 = sem("s_g2")
        s_y = sem("s_y")
        s_sid = sem("s_sid")
        s_tick = sem("s_tick")
        s_add = sem("s_add")
        N_CONST, N_MID, N_RC = 12, 8, 5
        CHAIN = TB + 1
        BX, BT1, BT2, BL1, BL2, BL3 = 0, 1, 2, 3, 4, 5

        block = outer.enter_context(nc.Block())

        def filled(eng, name, b):
            i, k = plan[name]
            eng.wait_ge(full[i], b * uses[i] + (k + 1))

        def drained(eng, name, b):
            i, k = plan[name]
            eng.wait_ge(free[i], b * uses[i] + (k + 2))

        def vacant(eng, name, b, after=()):
            least = {plan[name][0]: plan[name][1] + 1}
            for other in after:
                i, k = plan[other]
                least[i] = max(least.get(i, 0), k + 2)
            for i, v in least.items():
                eng.wait_ge(free[i], b * uses[i] + v)

        def at(name):
            return bank[plan[name][0]]

        def done(ins, name):
            ins.then_inc(full[plan[name][0]], 1)

        def taken(ins, name):
            ins.then_inc(free[plan[name][0]], 1)

        def on_act(t):
            return t % 4 == 3

        before_b = [B * uses[i] for i in range(8)]
        PRE_BANK, TOT_BANK, ID_BANK = 0, 1, 2
        b_uses = [1, 1, 1, 0, 0, 0, 0, 0]
        before_c = [before_b[i] + b_uses[i] for i in range(8)]

        @block.sync
        def _(sp):
            sp.dma_start(itok_sb[:, :], itok).then_inc(s_const, 16)
            sp.dma_start(wq_raw[:, :, :], wq).then_inc(s_const, 16)
            sp.dma_start(wk_sb[:, :, :], wk).then_inc(s_const, 16)
            sp.dma_start(wv_sb[:, :, :], wv).then_inc(s_const, 16)
            sp.dma_start(wo_sb[:, :, :], wo).then_inc(s_const, 16)
            sp.dma_start(wi_base[:, :, :], wi_t).then_inc(s_const, 16)
            sp.dma_start(wf_base[:, :, :], wo_t).then_inc(s_const, 16)
            sp.dma_start(lora[0:R, :], lora_c).then_inc(s_const, 16)
            sp.dma_start(id_f[:, :], ident).then_inc(s_const, 16)
            sp.dma_start(mask_f[:, :], maskd).then_inc(s_const, 16)
            sp.dma_start(low_sb[:, :], low).then_inc(s_const, 16)
            sp.dma_start(gw_sb[:, :, :], gate_w).then_inc(s_const, 16)
            sp.wait_ge(s_const, 16 * N_CONST)

            def expert_of(b):
                return sp.value_load(itok_sb[0:1, bass.ds(b, 1)], min_val=0, max_val=NE - 1)

            def load_in(b, e):
                sp.dma_start(x_in[:, :, :], xT[bass.ds(b, 1), :, :, :].rearrange("o p k t -> (o p) k t")
                             ).then_inc(s_in, 16)
                sp.dma_start(wc_sb[:, :, :], x_cond_w[bass.ds(e, 1), :, :, :].rearrange("o p k t -> (o p) k t")
                             ).then_inc(s_in, 16)
                sp.dma_start(bc_sb[:, :], x_cond_b[bass.ds(e, 1), :, :].rearrange("o p k -> (o p) k")
                             ).then_inc(s_in, 16)

            def load_lora(e):
                sp.dma_start(lora[R:2 * R, :], lora_e[bass.ds(e, 1), :, :].rearrange("o r n -> (o r) n")
                             ).then_inc(s_lora, 16)

            def load_res(b):
                sp.dma_start(x_res[:, :, :], xT[bass.ds(b, 1), :, :, :].rearrange("o p k t -> (o p) k t")
                             ).then_inc(s_xres, 16)

            def value(b, name, more):
                i, k = plan[name]
                return sp.snap(b * uses[i] + (k + more)) if not isinstance(b, int) else b * uses[i] + k + more

            def store(b, v_x1, v_hdone):
                for t2 in range(TB // 2):
                    sp.wait_ge(free[plan[("x1", t2)][0]], v_x1[t2])
                    sp.sem_inc(s_tick, 1)
                sp.dma_start(out[bass.ds(b, 1), :, :].rearrange("o (t p) d -> p (o t) d", p=P),
                             x1_sb[:, :, :]).then_inc(s_x1out, 16)
                sp.wait_ge(s_hdone, v_hdone)
                sp.sem_inc(s_tick, 1)
                sp.dma_start(hrows[bass.ds(b * S, S), :].rearrange("(t p) d -> p t d", p=P),
                             h_sb[:, :, :]).then_inc(s_hout, 16)

            e0 = expert_of(0)
            load_in(0, e0)
            load_lora(e0)
            load_res(0)
            sp.dma_start(gb_sb[:, :], gate_b.partition_broadcast(P)).then_inc(s_mid, 16)
            sp.dma_start(b3_sb[:, :, :].rearrange("p e d -> p (e d)"), b3.partition_broadcast(P)).then_inc(s_mid, 16)
            for e in range(NE):
                sp.dma_start(w1_sb[:, e, :, :], w1[e]).then_inc(s_w1, 16)
            with sp.Fori(0, B - 1) as b:
                b1_ = sp.snap(b + 1)
                e = expert_of(b1_)
                v_read = value(b, ("cond", KD - 1), 1)
                v_cond = [value(b, ("cond", o), 2) for o in range(KD)]
                v_fold = value(b, ("fold_o", KF // 2 - 1), 1)
                v_x1t = [value(b, ("x1t", o), 2) for o in range(KD)]
                v_x1 = [value(b, ("x1", t2), 2) for t2 in range(TB // 2)]
                sp.wait_ge(full[plan[("cond", KD - 1)][0]], v_read)
                sp.sem_inc(s_tick, 1)
                for o in range(KD):
                    sp.wait_ge(free[plan[("cond", o)][0]], v_cond[o])
                    sp.sem_inc(s_tick, 1)
                load_in(b1_, e)
                sp.wait_ge(full[plan[("fold_o", KF // 2 - 1)][0]], v_fold)
                sp.sem_inc(s_tick, 1)
                load_lora(e)
                for o in range(KD):
                    sp.wait_ge(free[plan[("x1t", o)][0]], v_x1t[o])
                    sp.sem_inc(s_tick, 1)
                load_res(b1_)
                store(b, v_x1, b1_)
            store(B - 1, [value(B - 1, ("x1", t2), 2) for t2 in range(TB // 2)], B)
            sp.wait_ge(s_x1out, 16 * B + 1)
            sp.wait_ge(s_hout, 16 * B + 1)
            for i in range(8):
                sp.wait_ge(full[i], before_b[i])
                sp.wait_ge(free[i], before_b[i] + 1)
            sp.dma_start(tri_f[:, :], tri).then_inc(s_rconst, 16)
            sp.dma_start(iota_r_sb[:, :], iota_r).then_inc(s_rconst, 16)
            sp.dma_start(iota_t_sb[:, :], iota_t).then_inc(s_rconst, 16)
            sp.dma_start(tok_sb[:, :, :], tok).then_inc(s_rconst, 16)
            sp.dma_start(thr_sb[:, :], thr).then_inc(s_rconst, 16)
            sp.dma_start(b1_sb[:, :, :].rearrange("p e d -> p (e d)"), b1.partition_broadcast(P)).then_inc(s_w23, 16)
            sp.dma_start(b2_sb[:, :, :].rearrange("p e d -> p (e d)"), b2.partition_broadcast(P)).then_inc(s_w23, 16)
            for e in range(NE):
                sp.dma_start(w2_sb[:, e, :, :], w2[e]).then_inc(s_w23, 16)
                sp.dma_start(w3_sb[:, e, :, :], w3[e]).then_inc(s_w23, 16)
            sp.wait_ge(s_add, 16 * TILES)

        @block.tensor
        def _(pe):
            for i in range(8):
                pe.sem_inc(free[i], 1)

            def mm(*a, **k):
                return nc.tensor.matmul(*a, **k)

            def batch(b):
                pe.wait_ge(s_in, b * 48 + 48)
                for o in range(KD):
                    n = ("cond", o)
                    vacant(pe, n, b)
                    for k in range(KD):
                        ins = mm(at(n)[:, :], wc_sb[:, k, o * P:(o + 1) * P], x_in[:, k, :],
                                 start=(k == 0), stop=(k == KD - 1))
                    done(ins, n)
                for c in range(HC):
                    for what, w in (("q", wq_raw), ("k", wk_sb)):
                        n = (what, c)
                        vacant(pe, n, b, [("cond", o) for o in range(KD)] if n == ("q", 0) else ())
                        for k in range(KD):
                            ins = mm(at(n)[:, :], w[:, k, c * P:(c + 1) * P], cond[:, k, :],
                                     start=(k == 0), stop=(k == KD - 1))
                        done(ins, n)
                for t2 in range(TB // 2):
                    n = ("v", t2)
                    vacant(pe, n, b)
                    for u in range(2):
                        t = 2 * t2 + u
                        for k in range(KD):
                            ins = mm(at(n)[:, u * D:(u + 1) * D], cond[:, k, t * P:(t + 1) * P], wv_sb[:, k, :],
                                     start=(k == 0), stop=(k == KD - 1))
                    done(ins, n)
                qkv = [(w, c) for c in range(HC) for w in "qk"] + [("v", t2) for t2 in range(TB // 2)]
                for step in range(STEPS):
                    ss, ts, pvs, _, rt, _ = units_at(step)
                    for s in ss:
                        w = (s // HEADS + 1) * P
                        vacant(pe, ("s", s), b, qkv if s == 0 else ())
                        mm(at(("s", s))[:, w - P:w], id_b[:, :], mask_b[:, :], start=True, stop=False,
                           skip_group_check=True)
                    for s in ss:
                        i, h = divmod(s, HEADS)
                        c, r = h // 4, STRIP * (h % 4)
                        n = ("s", s)
                        w = (i + 1) * P
                        q = q_sb[r:r + STRIP, c, i * P:(i + 1) * P]
                        mm(at(n)[:, 0:w], q, kh_sb[r:r + STRIP, c, 0:w], start=False, stop=False,
                           skip_group_check=True)
                        done(mm(at(n)[:, 0:w], q, kl_sb[r:r + STRIP, c, 0:w], start=False, stop=True,
                                skip_group_check=True), n)
                    for pv in pvs:
                        i, h = divmod(pv, HEADS)
                        n = ("pv", i)
                        if h == 0:
                            vacant(pe, n, b, [("t", pv)])
                        else:
                            drained(pe, ("t", pv), b)
                        r, col = STRIP * (h % 8 // 2), P * (h // 8)
                        for kb in range(i + 1):
                            ins = mm(at(n)[r:r + STRIP, col:col + P],
                                     v_sb[:, kb, h // 2, h % 2, :, :].rearrange("p a d -> p (a d)"),
                                     probs_t[:, pv % 4, kb * P:(kb + 1) * P],
                                     start=(h % 2 == 0 and kb == 0), stop=(h % 2 == 1 and kb == i))
                        if h == HEADS - 1:
                            done(ins, n)
                    for t in ts:
                        n = ("t", t)
                        vacant(pe, n, b, [("s", t)])
                        for kb in range(t // HEADS + 1):
                            ins = nc.tensor.transpose(at(n)[:, kb * P:(kb + 1) * P],
                                                      probs[:, t % 4, kb * P:(kb + 1) * P], id_f[:, :])
                        done(ins, n)
                    if rt is not None:
                        n = ("rt", rt)
                        pe.wait_ge(s_rrep, b * TB + (rt + 1))
                        vacant(pe, n, b)
                        for k in range(KD):
                            ins = nc.tensor.transpose(at(n)[:, k * P:(k + 1) * P],
                                                      rrep[:, k * P:(k + 1) * P], id_f[:, :])
                        done(ins, n)
                pe.wait_ge(s_lora, b * 16 + 16)
                for n4 in range(2 * KD):
                    n = ("fold_i", n4)
                    k, fh = n4 // 2, n4 % 2
                    vacant(pe, n, b)
                    done(mm(at(n)[:, :], lora[:, k * P:(k + 1) * P], lora[:, D + fh * 512:D + (fh + 1) * 512],
                            start=True, stop=True), n)
                for o in range(KD):
                    n = ("x1t", o)
                    vacant(pe, n, b, [("pv", i) for i in range(TB)] if o == 0 else ())
                    for k in range(KD):
                        ins = mm(at(n)[:, :], wo_sb[:, k, o * P:(o + 1) * P], ot_sb[:, k, :],
                                 start=(k == 0), stop=(k == KD - 1))
                    done(ins, n)
                for n4 in range(KF // 2):
                    n = ("fold_o", n4)
                    vacant(pe, n, b)
                    for u in range(2):
                        j = 2 * n4 + u
                        ins = mm(at(n)[:, u * D:(u + 1) * D], lora[:, D + F + j * P:D + F + (j + 1) * P],
                                 lora[:, D + 2 * F:D + 2 * F + D], start=True, stop=True)
                    done(ins, n)
                for j in range(KF):
                    n = ("hid", j)
                    vacant(pe, n, b, [("fold_i", n4) for n4 in range(2 * KD)] + [("x1t", o) for o in range(KD)] if j == 0 else ())
                    for k in range(KD):
                        ins = mm(at(n)[:, :], wi_eff[:, k, j * P:(j + 1) * P], x1t[:, k, :],
                                 start=(k == 0), stop=(k == KD - 1))
                    done(ins, n)
                for t2 in range(TB // 2):
                    n = ("x1", t2)
                    vacant(pe, n, b)
                    for u in range(2):
                        t = 2 * t2 + u
                        for k in range(KD):
                            ins = nc.tensor.transpose(at(n)[:, u * D + k * P:u * D + (k + 1) * P],
                                                      x1t[:, k, t * P:(t + 1) * P], id_f[:, :])
                    done(ins, n)
                for t2 in range(TB // 2):
                    n = ("h", t2)
                    vacant(pe, n, b, [("fold_o", n4) for n4 in range(KF // 2)] + [("hid", 0)] if t2 == 0 else ())
                    for u in range(2):
                        t = 2 * t2 + u
                        for j in range(KF):
                            if t == 0 and j > 0:
                                drained(pe, ("hid", j), b)
                            ins = mm(at(n)[:, u * D:(u + 1) * D], hid[:, j, t * P:(t + 1) * P], wf_eff[:, j, :],
                                     start=(j == 0), stop=(j == KF - 1))
                    done(ins, n)
                for k in range(KD):
                    n = ("ht", k)
                    vacant(pe, n, b, [("h", t2) for t2 in range(TB // 2)] if k == 0 else ())
                    for t in range(TB):
                        ins = nc.tensor.transpose(at(n)[:, t * P:(t + 1) * P], h_sb[:, t, k * P:(k + 1) * P],
                                                  id_f[:, :])
                    done(ins, n)
                n = ("gate", 0)
                vacant(pe, n, b, [("ht", k) for k in range(KD)])
                for t in range(TB):
                    for k in range(KD):
                        ins = mm(at(n)[:, t * NE:(t + 1) * NE], ht_sb[:, k, t * P:(t + 1) * P], gw_sb[:, k, :],
                                 start=(k == 0), stop=(k == KD - 1))
                done(ins, n)

            pe.wait_ge(s_const, 16 * N_CONST)
            pe.wait_ge(s_idb, 1)
            pe.wait_ge(s_vzero, 1)
            pe.wait_ge(s_prep, 1)
            with pe.Fori(0, B) as b:
                batch(b)

            pe.wait_ge(s_ohot, 1)
            pe.wait_ge(s_rconst, 16 * N_RC)
            pe.wait_ge(free[PRE_BANK], before_b[PRE_BANK] + 1)
            hots_flat = hots[:, :, :].rearrange("p t e -> p (t e)")
            mm(bank[PRE_BANK][:, 0:NT * NE], tri_sb[:, :], hots_flat, start=True, stop=True
               ).then_inc(full[PRE_BANK], 1)
            pe.wait_ge(free[TOT_BANK], before_b[TOT_BANK] + 1)
            mm(bank[TOT_BANK][:, 0:NT * NE], ones_b[:, :], hots_flat, start=True, stop=True
               ).then_inc(full[TOT_BANK], 1)
            pe.wait_ge(free[ID_BANK], before_b[ID_BANK] + 1)
            n = 0
            for c in range(2):
                for g in range(4):
                    pe.wait_ge(s_hit, 4 * c + g + 1)
                    for t in range(g * NT // 4, (g + 1) * NT // 4):
                        ins = mm(bank[ID_BANK][:, 0:2 * TILES], hit_r[:, t, :],
                                 hit_v[:, t % (NT // 4), :, :].rearrange("p a j -> p (a j)"),
                                 start=(n == 0), stop=(n == 2 * NT - 1))
                        n += 1
                    ins.then_inc(s_hitu, 1)
            pe.wait_ge(s_route, 1)
            pe.wait_ge(s_w1, 16 * NE)

            e_regs = [pe.alloc_register(f"pe_expert{d}") for d in range(AHEAD)]

            def experts(j):
                pe.load(e_regs, etab[0:1, bass.ds(max(j, 0), 1) if isinstance(j, int) else bass.ds(j, 1), :]
                         .rearrange("p o d -> p (o d)"))
                e = [pe.snap(reg, min_val=0, max_val=NE - 1) for reg in e_regs]
                return [None] * -j + e if isinstance(j, int) and j < 0 else e

            def up(i, j):
                return before_c[i] + 1 + j

            def x_trans(j):
                pe.wait_ge(s_xg, 16 * j + 16)
                pe.wait_ge(free[BX], up(BX, j))
                for k in range(KD):
                    ins = nc.tensor.transpose(bank[BX][:, k * P:(k + 1) * P], xg[:, k * P:(k + 1) * P], id_f[:, :])
                ins.then_inc(full[BX], 1)

            def layer1(j, e):
                pe.wait_ge(free[BX], up(BX, j) + 1)
                for k in range(KD):
                    ins = mm(bank[BL1][:, :], xgt[:, k, :],
                             w1_sb[:, bass.ds(e, 1), k, :].rearrange("p o n -> p (o n)"),
                             start=(k == 0), stop=(k == KD - 1))
                ins.then_inc(full[BL1], 1)

            def g_trans(j, g, s_g, bt):
                pe.wait_ge(s_g, j + 1)
                pe.wait_ge(free[bt], up(bt, j))
                for k in range(KH):
                    ins = nc.tensor.transpose(bank[bt][:, k * P:(k + 1) * P], g[:, k * P:(k + 1) * P], id_f[:, :])
                ins.then_inc(full[bt], 1)

            def layer2(j, e, half):
                if half == 0:
                    pe.wait_ge(free[BT1], up(BT1, j) + 1)
                for k in range(2 * half, 2 * half + 2):
                    ins = mm(bank[BL2][:, :], g1t[:, k, :],
                             w2_sb[:, bass.ds(e, 1), k, :].rearrange("p o n -> p (o n)"),
                             start=(k == 0), stop=(k == KH - 1))
                if half == 1:
                    ins.then_inc(full[BL2], 1)

            def layer3(j, e):
                pe.wait_ge(free[BT2], up(BT2, j) + 1)
                pe.wait_ge(free[BL3], up(BL3, j))
                for k in range(KH):
                    ins = mm(bank[BL3][:, 0:D], g2t[:, k, :],
                             w3_sb[:, bass.ds(e, 1), k, :].rearrange("p o n -> p (o n)"),
                             start=(k == 0), stop=(k == KH - 1))
                ins.then_inc(full[BL3], 1)

            def step(j, has):
                e = experts(j)
                if has(2):
                    layer1(j + 2, e[2])
                if has(0):
                    g_trans(j, g2, s_g2, BT2)
                if has(1):
                    layer2(j + 1, e[1], 0)
                if has(0):
                    layer3(j, e[0])
                if has(3):
                    x_trans(j + 3)
                if has(1):
                    layer2(j + 1, e[1], 1)
                if has(2):
                    g_trans(j + 2, g1, s_g1, BT1)

            for j in (-3, -2):
                step(j, lambda d: 0 <= j + d)
            pe.wait_ge(s_w23, 16 * (2 + 2 * NE))
            step(-1, lambda d: -1 + d >= 0)
            with pe.Fori(0, TILES - 3) as j:
                step(j, lambda d: True)
            for j in range(TILES - 3, TILES):
                step(j, lambda d: j + d < TILES)

        @block.scalar
        def _(act):
            act.wait_ge(s_const, 16 * N_CONST)
            nc.scalar.copy(id_b[:, :], id_f[:, :])
            nc.scalar.copy(mask_b[:, :], mask_f[:, :]).then_inc(s_idb, 1)
            act.wait_ge(s_vzero, 1)
            act.sem_inc(s_x1out, 1)

            def batch(b):
                act.wait_ge(s_in, b * 48 + 48)
                for o in range(KD):
                    n = ("cond", o)
                    filled(act, n, b)
                    taken(nc.scalar.activation(cond[:, o, :], at(n)[:, :], ACT.Identity, bias=bc_sb[:, o:o + 1]), n)
                for c in range(HC):
                    filled(act, ("q", c), b)
                    if c > 0:
                        drained(act, ("q", c - 1), b)
                    nc.scalar.copy(q_hi[:, :], at(("q", c))[:, :]).then_inc(s_hi, 1)
                    filled(act, ("k", c), b)
                    nc.scalar.copy(kh_sb[:, c, :], at(("k", c))[:, :]).then_inc(s_hi, 1)
                for t2 in range(TB // 2):
                    n = ("v", t2)
                    filled(act, n, b)
                    v_ps = at(n)[:, :].rearrange("p (t s e d) -> p t s e d", t=2, e=2, d=DH)
                    nc.scalar.copy(v_sb[:, 2 * t2:2 * t2 + 2, :, 0, 0, :], v_ps[:, :, :, 0, :])
                    taken(nc.scalar.copy(v_sb[:, 2 * t2:2 * t2 + 2, :, 1, 1, :], v_ps[:, :, :, 1, :]), n)
                for step in range(STEPS):
                    ss, ts, _, _, rt, _ = units_at(step)
                    for s in ss:
                        i, h = divmod(s, HEADS)
                        n = ("s", s)
                        act.wait_ge(s_max, b * UNITS + (s + 1))
                        if h == 0 and i >= 2:
                            act.wait_ge(s_rrep, b * TB + (i - 1))
                        taken(nc.scalar.activation(probs[:, s % 4, 0:(i + 1) * P], at(n)[:, 0:(i + 1) * P], ACT.Exp,
                                                   bias=nmax[:, s % 8:s % 8 + 1], accum_out=rsum[:, i % 2, h:h + 1]), n)
                    for t in ts:
                        if on_act(t):
                            n = ("t", t)
                            w = (t // HEADS + 1) * P
                            filled(act, n, b)
                            taken(nc.scalar.copy(probs_t[:, t % 4, 0:w], at(n)[:, 0:w]), n)
                    if rt is not None:
                        n = ("rt", rt)
                        filled(act, n, b)
                        if rt > 0:
                            drained(act, ("pv", rt - 1), b)
                        taken(nc.scalar.copy(rt_sb[:, :], at(n)[:, 0:D]), n)
                for j in range(0, KF, 2):
                    n = ("hid", j)
                    filled(act, n, b)
                    taken(nc.scalar.activation(hid[:, j, :], at(n)[:, :], ACT.Relu), n)
                act.wait_ge(s_x1out, b * 16 + 1)
                for t2 in range(TB // 2):
                    n = ("x1", t2)
                    filled(act, n, b)
                    taken(nc.scalar.copy(x1_sb[:, 2 * t2:2 * t2 + 2, :].rearrange("p t d -> p (t d)"), at(n)[:, :]), n)
                n = ("ht", 1)
                filled(act, n, b)
                taken(nc.scalar.copy(ht_sb[:, 1, :], at(n)[:, :]), n)
                act.wait_ge(s_gneg, b + 1)
                nc.scalar.activation(gexp[:, :, :], gexp[:, :, :], ACT.Exp).then_inc(s_gexp, 1)

            with act.Fori(0, B) as b:
                batch(b)

            def gelu(j, z, g, s_z, s_g):
                act.wait_ge(s_z, j + 1)
                nc.scalar.activation(g[:, :], z[:, :], ACT.Gelu).then_inc(s_g, 1)

            def step(j, has):
                if has(2):
                    gelu(j + 2, z1, g1, s_z1, s_g1)
                if has(1):
                    gelu(j + 1, z2, g2, s_z2, s_g2)

            for j in (-2, -1):
                step(j, lambda d: 0 <= j + d)
            with act.Fori(0, TILES - 2) as j:
                step(j, lambda d: True)
            for j in range(TILES - 2, TILES):
                step(j, lambda d: j + d < TILES)

        @block.vector
        def _(dve):
            V = nc.vector
            dve.wait_ge(s_const, 16 * N_CONST)
            V.tensor_scalar(wq_raw[:, :, :].rearrange("p k n -> p (k n)"), wq_raw[:, :, :].rearrange("p k n -> p (k n)"),
                            DH ** -0.5, None, ALU.mult).then_inc(s_prep, 1)
            dve.sem_inc(s_hout, 1)
            dve.wait_ge(s_mid, 32)

            def fold(name, eff, base, b):
                filled(dve, name, b)
                taken(V.scalar_tensor_tensor(eff, at(name)[:, :], 2.0, base, ALU.mult, ALU.add), name)

            def batch(b):
                for c in range(HC):
                    dve.wait_ge(s_hi, b * (2 * HC) + (2 * c + 1))
                    n = ("q", c)
                    filled(dve, n, b)
                    taken(V.scalar_tensor_tensor(q_sb[:, c, :], q_hi[:, :].bitcast(F32), low_sb[:, 0:1], at(n)[:, :],
                                                 ALU.mult, ALU.add), n)
                    dve.wait_ge(s_hi, b * (2 * HC) + (2 * c + 2))
                    n = ("k", c)
                    filled(dve, n, b)
                    taken(V.scalar_tensor_tensor(kl_sb[:, c, :], kh_sb[:, c, :].bitcast(F32), -1.0, at(n)[:, :],
                                                 ALU.mult, ALU.add), n)
                for step in range(STEPS):
                    ss, ts, _, inv, _, norm = units_at(step)
                    for s in ss:
                        n = ("s", s)
                        filled(dve, n, b)
                        V.tensor_reduce(nmax[:, s % 8:s % 8 + 1], at(n)[:, 0:(s // HEADS + 1) * P], AX.X, ALU.max,
                                        negate=True).then_inc(s_max, 1)
                    for t in ts:
                        if not on_act(t):
                            n = ("t", t)
                            w = (t // HEADS + 1) * P
                            filled(dve, n, b)
                            taken(V.tensor_copy(probs_t[:, t % 4, 0:w], at(n)[:, 0:w]), n)
                    if inv is not None:
                        drained(dve, ("s", inv * HEADS + HEADS - 1), b)
                        V.reciprocal(rinv[:, :], rsum[:, inv % 2, :]).then_inc(s_chain, 1)
                        dve.wait_ge(s_chain, b * CHAIN + (inv + 1))
                        V.tensor_copy(rrep[:, :].rearrange("p (h d) -> p h d", d=DH),
                                      rinv[:, :].unsqueeze(2).to_broadcast([P, HEADS, DH])).then_inc(s_rrep, 1)
                    if norm is not None:
                        n = ("pv", norm)
                        drained(dve, ("rt", norm), b)
                        filled(dve, n, b)
                        taken(V.tensor_tensor(ot_sb[:, :, norm * P:(norm + 1) * P],
                                              at(n)[:, 0:D].rearrange("p (k t) -> p k t", k=KD),
                                              rt_sb[:, :].rearrange("p (k t) -> p k t", k=KD), ALU.mult), n)
                for n4 in range(2 * KD):
                    k, fh = n4 // 2, n4 % 2
                    fold(("fold_i", n4), wi_eff[:, k, fh * 512:(fh + 1) * 512],
                         wi_base[:, k, fh * 512:(fh + 1) * 512], b)
                dve.wait_ge(s_xres, b * 16 + 16)
                for o in range(KD):
                    n = ("x1t", o)
                    filled(dve, n, b)
                    taken(V.tensor_tensor(x1t[:, o, :], at(n)[:, :], x_res[:, o, :], ALU.add), n)
                for n4 in range(KF // 2):
                    fold(("fold_o", n4), wf_eff[:, 2 * n4:2 * n4 + 2, :].rearrange("p j d -> p (j d)"),
                         wf_base[:, 2 * n4:2 * n4 + 2, :].rearrange("p j d -> p (j d)"), b)
                for j in range(1, KF, 2):
                    n = ("hid", j)
                    filled(dve, n, b)
                    taken(V.tensor_scalar(hid[:, j, :], at(n)[:, :], 0.0, None, ALU.max), n)
                dve.wait_ge(s_hout, b * 16 + 1)
                for t2 in range(TB // 2):
                    n = ("h", t2)
                    filled(dve, n, b)
                    taken(V.tensor_copy(h_sb[:, 2 * t2:2 * t2 + 2, 0:D],
                                        at(n)[:, :].rearrange("p (t d) -> p t d", d=D)), n)
                n = ("ht", 0)
                filled(dve, n, b)
                taken(V.tensor_copy(ht_sb[:, 0, :], at(n)[:, :]), n)
                n = ("gate", 0)
                filled(dve, n, b)
                taken(V.tensor_tensor(glog[:, :, :], at(n)[:, 0:TB * NE].rearrange("p (t e) -> p t e", e=NE),
                                      gb_sb[:, :].unsqueeze(1).to_broadcast([P, TB, NE]), ALU.add), n)
                drained(dve, n, b)
                V.tensor_copy(logits[:, bass.ds(b * TB, TB), :], glog[:, :, :])
                V.tensor_reduce(gmax[:, :], glog[:, :, :], AX.X, ALU.max).then_inc(s_chain, 1)
                dve.wait_ge(s_chain, b * CHAIN + (TB + 1))
                V.tensor_tensor(gexp[:, :, :], glog[:, :, :], gmax[:, :].unsqueeze(2).to_broadcast([P, TB, NE]),
                                ALU.subtract).then_inc(s_gneg, 1)
                dve.wait_ge(s_gexp, b + 1)
                V.tensor_reduce(gsum[:, :], gexp[:, :, :], AX.X, ALU.add).then_inc(s_gchain, 1)
                dve.wait_ge(s_gchain, 2 * b + 1)
                V.reciprocal(ginv[:, :], gsum[:, :]).then_inc(s_gchain, 1)
                dve.wait_ge(s_gchain, 2 * b + 2)
                V.tensor_tensor(h_sb[:, :, D:ROW], gexp[:, :, :], ginv[:, :].unsqueeze(2).to_broadcast([P, TB, NE]),
                                ALU.mult).then_inc(s_hdone, 1)

            with dve.Fori(0, B) as b:
                batch(b)

            links = [0]

            def link(ins):
                links[0] += 1
                ins.then_inc(s_rchain, 1)
                dve.wait_ge(s_rchain, links[0])

            def over_e(ap):
                return ap.unsqueeze(2).to_broadcast([P, NT, NE])

            dve.wait_ge(s_hout, 16 * B + 1)
            dve.wait_ge(s_x1out, 16 * B + 1)
            for i in range(8):
                dve.wait_ge(full[i], before_b[i])
                dve.wait_ge(free[i], before_b[i] + 1)
            dve.wait_ge(s_rconst, 16 * N_RC)
            link(V.memset(ones_b[:, :], 1.0))
            link(V.tensor_copy(tri_sb[:, :], tri_f[:, :]))
            for c in range(2):
                src = logits if c == 0 else lg2
                link(V.tensor_reduce(m1[:, :], src[:, :, :], AX.X, ALU.max))
                link(V.tensor_tensor(rk[:, :, :], src[:, :, :], over_e(m1[:, :]), ALU.is_equal))
                link(V.tensor_tensor(rk[:, :, :], rk[:, :, :],
                                     iota_t_sb[:, 1:NE + 1].unsqueeze(1).to_broadcast([P, NT, NE]), ALU.mult))
                link(V.tensor_scalar(run[0][:, :, :], rk[:, :, :], 0.0, 1000.0, ALU.is_equal, ALU.mult))
                link(V.tensor_tensor(rk[:, :, :], rk[:, :, :], run[0][:, :, :], ALU.add))
                link(V.tensor_reduce(m1[:, :], rk[:, :, :], AX.X, ALU.min))
                link(V.tensor_tensor(hot[c][:, :, :], rk[:, :, :], over_e(m1[:, :]), ALU.is_equal))
                if c == 0:
                    link(V.scalar_tensor_tensor(lg2[:, :, :].rearrange("p t e -> p (t e)"),
                                                hot[0][:, :, :].rearrange("p t e -> p (t e)"), -BIG,
                                                logits[:, :, :].rearrange("p t e -> p (t e)"), ALU.mult, ALU.add))
            V.tensor_tensor(hots[:, :, :], hot[0][:, :, :], hot[1][:, :, :], ALU.add).then_inc(s_ohot, 1)
            dve.wait_ge(full[TOT_BANK], before_b[TOT_BANK] + 1)
            link(V.tensor_copy(run[0][:, :, :].rearrange("p t e -> p (t e)"), bank[TOT_BANK][:, 0:NT * NE]))
            cur = 0
            for sh in (1, 2, 4, 8, 16):
                link(V.tensor_copy(run[1 - cur][:, 0:sh, :], run[cur][:, 0:sh, :]))
                link(V.tensor_tensor(run[1 - cur][:, sh:NT, :], run[cur][:, sh:NT, :], run[cur][:, 0:NT - sh, :], ALU.add))
                cur = 1 - cur
            link(V.tensor_copy(cnt[:, :], run[cur][:, NT - 1, :]))
            link(V.tensor_tensor(run[1 - cur][:, :, :].rearrange("p t e -> p (t e)"),
                                 run[cur][:, :, :].rearrange("p t e -> p (t e)"), bank[TOT_BANK][:, 0:NT * NE],
                                 ALU.subtract))
            dve.sem_inc(free[TOT_BANK], 1)
            dve.wait_ge(full[PRE_BANK], before_b[PRE_BANK] + 1)
            V.tensor_tensor(pre[:, :, :].rearrange("p t e -> p (t e)"),
                            run[1 - cur][:, :, :].rearrange("p t e -> p (t e)"), bank[PRE_BANK][:, 0:NT * NE],
                            ALU.add).then_inc(free[PRE_BANK], 1)
            dve.wait_ge(free[PRE_BANK], before_b[PRE_BANK] + 2)
            link(V.tensor_tensor(cmpt[:, :, :], cnt[:, :].unsqueeze(2).to_broadcast([P, NE, 2 * NT]),
                                 thr_sb[:, :].unsqueeze(1).to_broadcast([P, NE, 2 * NT]), ALU.is_gt))
            link(V.tensor_reduce(ntile[:, :], cmpt[:, :, :], AX.X, ALU.add))
            link(V.memset(tbase[:, :], 0.0))
            for e in range(NE):
                link(V.tensor_tensor(tbase[:, e + 1:e + 2], tbase[:, e:e + 1], ntile[:, e:e + 1], ALU.add))
            link(V.memset(eacc[0][:, :], 0.0))
            ecur = 0
            for e in range(1, NE):
                link(V.scalar_tensor_tensor(eacc[1 - ecur][:, :], iota_t_sb[0:1, 0:TILES], tbase[0:1, e:e + 1],
                                            eacc[ecur][:, :], ALU.is_ge, ALU.add))
                ecur = 1 - ecur
            link(V.memset(etab[:, :, :], 0))
            for d in range(AHEAD):
                link(V.tensor_copy(etab[:, 0:TILES - d, d], eacc[ecur][:, d:TILES]))
            link(V.scalar_tensor_tensor(pre[:, :, :], tbase[:, 0:NE].unsqueeze(1).to_broadcast([P, NT, NE]), float(P),
                                        pre[:, :, :], ALU.mult, ALU.add))
            n_hit = 0
            for c in range(2):
                link(V.tensor_tensor(rk[:, :, :], hot[c][:, :, :], pre[:, :, :], ALU.mult))
                link(V.tensor_reduce(slot[:, :], rk[:, :, :], AX.X, ALU.add))
                link(V.tensor_copy(s_i[:, 0, :], slot[:, :]))
                link(V.tensor_scalar(s_i[:, 1, :], s_i[:, 0, :], 7, None, ALU.arith_shift_right))
                link(V.tensor_copy(s_j[:, c, :], s_i[:, 1, :]))
                link(V.scalar_tensor_tensor(s_r[:, c, :], s_j[:, c, :], -float(P), slot[:, :], ALU.mult, ALU.add))
                if c == 1:
                    dve.wait_ge(s_hitu, 4)
                link(V.tensor_tensor(hit_r[:, :, :], iota_r_sb[:, :].unsqueeze(1).to_broadcast([P, NT, P]),
                                     s_r[:, c, :].unsqueeze(2).to_broadcast([P, NT, P]), ALU.is_equal))
                for g in range(4):
                    q = NT // 4
                    ts_ = slice(g * q, (g + 1) * q)
                    if n_hit > 0:
                        dve.wait_ge(s_hitu, n_hit)
                    link(V.tensor_tensor(hit_j[:, :, :], iota_t_sb[:, 0:TILES].unsqueeze(1).to_broadcast([P, q, TILES]),
                                         s_j[:, c, ts_].unsqueeze(2).to_broadcast([P, q, TILES]), ALU.is_equal))
                    for a in range(2):
                        ins = V.tensor_tensor(hit_v[:, :, a, :], hit_j[:, :, :],
                                              tok_sb[:, ts_, a].unsqueeze(2).to_broadcast([P, q, TILES]), ALU.mult)
                        if a == 0:
                            link(ins)
                        else:
                            ins.then_inc(s_hit, 1)
                            dve.wait_ge(s_hit, n_hit + 1)
                    n_hit += 1
            dve.wait_ge(s_hitu, 8)
            link(V.tensor_copy(ids_f[:, :], bank[ID_BANK][:, 0:TILES]))
            V.tensor_tensor(ids_g[:, :], ids_f[:, :], bank[ID_BANK][:, TILES:2 * TILES], ALU.add
                            ).then_inc(free[ID_BANK], 1)
            dve.wait_ge(free[ID_BANK], before_b[ID_BANK] + 2)
            link(V.tensor_scalar(ids_f[:, :], ids_g[:, :], -1.0, 0.0, ALU.add, ALU.max))
            link(V.tensor_copy(gather_id[:, :], ids_f[:, :]))
            link(V.tensor_scalar(ids_f[:, :], ids_g[:, :], 0.0, float(2 * B * S), ALU.is_equal, ALU.mult))
            link(V.scalar_tensor_tensor(ids_f[:, :], ids_g[:, :], -1.0, ids_f[:, :], ALU.add, ALU.add))
            V.tensor_copy(scatter_id[:, :], ids_f[:, :]).then_inc(s_route, 1)
            dve.wait_ge(s_route, 1)
            dve.wait_ge(s_w23, 16 * (2 + 2 * NE))

            e_regs = [dve.alloc_register(f"dve_expert{d}") for d in range(AHEAD)]

            def experts(j):
                dve.load(e_regs, etab[0:1, bass.ds(max(j, 0), 1) if isinstance(j, int) else bass.ds(j, 1), :]
                         .rearrange("p o d -> p (o d)"))
                e = [dve.snap(reg, min_val=0, max_val=NE - 1) for reg in e_regs]
                return [None] * -j + e if isinstance(j, int) and j < 0 else e

            def up(i, j):
                return before_c[i] + 1 + j

            def fl(i, j):
                return before_b[i] + (1 if i < 2 else 0) + 1 + j

            def x_evac(j, e):
                dve.wait_ge(s_xg, 16 * j + 16)
                V.tensor_copy(wsel[:, bass.ds(j, 1)], xg[:, bass.ds(e + D, 1)]).then_inc(s_wsel, 1)
                dve.wait_ge(full[BX], fl(BX, j))
                V.tensor_copy(xgt[:, :, :].rearrange("p k t -> p (k t)"), bank[BX][:, 0:D]).then_inc(free[BX], 1)

            def add_bias(j, e, bl, z, bias, s_z):
                dve.wait_ge(full[bl], fl(bl, j))
                V.tensor_tensor(z[:, :], bank[bl][:, :], bias[:, bass.ds(e, 1), :].rearrange("p o n -> p (o n)"),
                                ALU.add).then_inc(s_z, 1)

            def t_evac(j, bt, gt):
                dve.wait_ge(full[bt], fl(bt, j))
                V.tensor_copy(gt[:, :, :].rearrange("p k t -> p (k t)"), bank[bt][:, :]).then_inc(free[bt], 1)

            def first(d):
                return True

            def step(j, has):
                e = experts(j)
                if has(2):
                    add_bias(j + 2, e[2], BL1, z1, b1_sb, s_z1)
                if has(0):
                    t_evac(j, BT2, g2t)
                    dve.wait_ge(full[BL3], fl(BL3, j))
                    V.tensor_tensor(y0[:, :], bank[BL3][:, 0:D], b3_sb[:, bass.ds(e[0], 1), :].rearrange("p o n -> p (o n)"),
                                    ALU.add).then_inc(free[BL3], 1)
                    dve.wait_ge(free[BL3], up(BL3, j) + 1)
                    if has is not first:
                        dve.wait_ge(s_add, 16 * j)
                    V.tensor_scalar(y_sb[:, :], y0[:, :], wsel[:, bass.ds(j, 1)], None, ALU.mult).then_inc(s_y, 1)
                if has(3):
                    x_evac(j + 3, e[3])
                if has(1):
                    add_bias(j + 1, e[1], BL2, z2, b2_sb, s_z2)
                if has(2):
                    t_evac(j + 2, BT1, g1t)

            for j in (-3, -2, -1):
                step(j, lambda d: 0 <= j + d)
            step(0, first)
            with dve.Fori(1, TILES - 3) as j:
                step(j, lambda d: True)
            for j in range(TILES - 3, TILES):
                step(j, lambda d: j + d < TILES)

        @block.gpsimd
        def _(pool):
            nc.gpsimd.memset(v_sb[:, :, :, :, :, :].rearrange("p t s e a d -> p (t s e a d)"), 0.0).then_inc(s_vzero, 1)
            pool.wait_ge(s_route, 1)
            pool.wait_ge(s_hout, 16 * B + 1)
            pool.wait_ge(s_x1out, 16 * B + 1)

            def gather(j, vj1):
                nc.gpsimd.tensor_copy(gid[:, :], gather_id[:, bass.ds(j, 1)]).then_inc(s_gid, 1)
                pool.wait_ge(s_gid, vj1)
                pool.sem_inc(s_tick, 1)
                nc.gpsimd.indirect_dma_start(
                    xg[:, :], None, hrows, bass.IndirectOffsetOnAxis(ap=gid[:, 0:1], axis=0),
                    bounds_check=B * S - 1, oob_is_err=False).then_inc(s_xg, 16)

            def scatter(j, vj1):
                nc.gpsimd.tensor_copy(sid[:, :], scatter_id[:, bass.ds(j, 1)]).then_inc(s_sid, 1)
                pool.wait_ge(s_sid, vj1)
                pool.wait_ge(s_y, vj1)
                pool.sem_inc(s_tick, 1)
                nc.gpsimd.indirect_dma_start(
                    out_rows, bass.IndirectOffsetOnAxis(ap=sid[:, 0:1], axis=0), y_sb[:, :], None,
                    bounds_check=B * S - 1, oob_is_err=False, compute_op=ALU.add).then_inc(s_add, 16)

            def xg_free(v_bank, v_sel):
                pool.wait_ge(full[BX], v_bank)
                pool.sem_inc(s_tick, 1)
                pool.wait_ge(s_wsel, v_sel)
                pool.sem_inc(s_tick, 1)

            filled_x = before_b[BX] + b_uses[BX]
            gather(0, 1)
            for j in range(3):
                xg_free(filled_x + j + 1, j + 1)
                gather(j + 1, j + 2)
            scatter(0, 1)
            xg_free(filled_x + 4, 4)
            gather(4, 5)
            with pool.Fori(1, TILES - 4) as j:
                v_added, v_j1, v_j4, v_j5 = (pool.snap(v) for v in (16 * j, j + 1, j + 4, j + 5))
                v_bx = pool.snap(j + (filled_x + 4))
                pool.wait_ge(s_add, v_added)
                scatter(j, v_j1)
                xg_free(v_bx, v_j4)
                gather(v_j4, v_j5)
            for j in range(TILES - 4, TILES):
                pool.wait_ge(s_add, 16 * j)
                scatter(j, j + 1)


_OUTS = [((B, S, D), "float32")]


def kernel(**inputs):
    import numpy as _np
    import concourse.bacc as _bacc
    from concourse import mybir as _mybir
    from concourse.bass_utils import run_bass_kernel_spmd as _run

    def chunked(w):
        n, k, m = w.shape
        return w.reshape(n, k // P, P, m).transpose(0, 2, 1, 3)

    def get(name):
        return _np.asarray(inputs[name])

    def strips(w):
        w = w.reshape(D, HEADS, DH)
        return chunked(_np.concatenate([w, w], axis=2).reshape(1, D, HEADS * 2 * DH))[0]

    def lora_rows(wi_a, wi_b, wo_a, wo_b):
        return _np.concatenate([wi_a, wi_b.swapaxes(-1, -2), wo_a, wo_b.swapaxes(-1, -2)], axis=-1)

    iota = _np.arange(P, dtype=_np.float32)
    tokens = (_np.arange(NT)[None, :] * P + _np.arange(P)[:, None] + 1)
    data = {
        "xT": chunked(get("x").transpose(0, 2, 1)),
        "cond_w": chunked(get("L0_cond_weight").transpose(0, 2, 1)),
        "cond_b": get("L0_cond_bias").reshape(NE, KD, P).transpose(0, 2, 1),
        "itok": get("itok_B_0_7").reshape(1, B),
        "wq": strips(get("L0_attn_W_Q")),
        "wk": strips(get("L0_attn_W_K")),
        "wv": chunked(get("L0_attn_W_V")[None])[0],
        "wo": chunked(get("L0_attn_W_o")[None])[0],
        "wi_t": chunked(get("L0_cond2_wi").T[None])[0],
        "wo_t": chunked(get("L0_cond2_wo").T[None])[0],
        "lora_c": lora_rows(*(get("L0_cond2_common_" + n) for n in ("wi_a", "wi_b", "wo_a", "wo_b"))),
        "lora_e": lora_rows(*(get("L0_cond2_experts_" + n) for n in ("wi_a", "wi_b", "wo_a", "wo_b"))),
        "gate_w": chunked(get("L0_ffn_gate_w")[None])[0],
        "gate_b": get("L0_ffn_gate_b").reshape(NE),
        "w1": chunked(get("L0_ffn_w1")),
        "w2": chunked(get("L0_ffn_w2")),
        "w3": chunked(get("L0_ffn_w3")),
        "b1": get("L0_ffn_b1").reshape(NE * H),
        "b2": get("L0_ffn_b2").reshape(NE * H),
        "b3": get("L0_ffn_b3").reshape(NE * D),
        "ident": _np.eye(P, dtype=_np.float32),
        "maskd": _np.triu(_np.full((P, P), -BIG, _np.float32), 1),
        "tri": _np.triu(_np.ones((P, P), _np.float32), 1),
        "low": -((_np.arange(P) % STRIP) >= DH).astype(_np.float32).reshape(P, 1),
        "iota_r": _np.tile(iota, (P, 1)),
        "iota_t": _np.tile(_np.arange(TILES, dtype=_np.float32), (P, 1)),
        "tok": _np.stack([tokens % 64, tokens - tokens % 64], axis=2).astype(_np.float32),
        "thr": _np.tile(_np.arange(2 * NT, dtype=_np.float32) * P, (P, 1)),
    }
    nc = _bacc.Bacc("TRN2", target_bir_lowering=False, num_devices=1)
    arrays, args = {}, []
    for name, a in data.items():
        a = _np.ascontiguousarray(a)
        arrays[f"in_{name}"] = a
        args.append(nc.dram_tensor(f"in_{name}", a.shape, _mybir.dt.from_np(a.dtype), kind="ExternalInput").ap())
    for i, (shape, dtype) in enumerate(_OUTS):
        dt = _mybir.dt.from_np(_np.dtype(dtype))
        args.append(nc.dram_tensor(f"out_{i}", shape, dt, kind="ExternalOutput").ap())
    build_kernel(nc, *args)
    r = _run(nc, [arrays], core_ids=[0])
    return r.results[0]["out_0"]
```

```python
from contextlib import ExitStack

import concourse.bass as bass
from concourse import mybir

F32 = mybir.dt.float32
F32R = mybir.dt.float32r
BF16 = mybir.dt.bfloat16
I32 = mybir.dt.int32
U32 = mybir.dt.uint32
ALU = mybir.AluOpType
ACT = mybir.ActivationFunctionType
AX = mybir.AxisListType

P = 128
B, S, D = 8, 512, 256
KD = D // P
TB = S // P
HEADS, DH = 16, 16
STRIP = 64
HC = HEADS * STRIP // P
PART = 32
F = 1024
KF = F // P
R = 16
LORA = D + F + F + D
NE = 8
H = 512
KH = H // P
NT = B * TB
ROW = D + NE
AHEAD = 4
HIT_GROUP = NT // 4
TILES = (2 * B * S + NE * (P - 1)) // P
TW = TILES + TILES % 2
ROUTE_REST = 3240
BIG = 1.0e30
PV_BANK = 6
UNITS = TB * HEADS
PAIR = 2
T_LAG, PV_LAG = 1, 2
INV_LAG, RT_LAG, NORM_LAG = 1, 2, 3
STEPS = UNITS // PAIR + NORM_LAG


def units_at(step):
    def units(n):
        return range(PAIR * n, PAIR * n + PAIR) if 0 <= PAIR * n < UNITS else ()

    def tile(n):
        per = HEADS // PAIR
        return n // per if 0 <= n < UNITS // PAIR and n % per == per - 1 else None
    return (units(step), units(step - T_LAG), units(step - PV_LAG),
            tile(step - INV_LAG), tile(step - RT_LAG), tile(step - NORM_LAG))


HID_EARLY = 4
H_PIECES = 4
FILLERS = ([(("hid", j), k) for j in range(HID_EARLY, KF) for k in range(KD)] +
           [(None, 0)] + [(("x1", t2), 0) for t2 in range(TB // 2)] +
           [(("h", t), piece) for t in range(TB) for piece in range(H_PIECES)] +
           [(("next", o), k) for o in range(KD) for k in range(KD)] +
           [(("ht", k), 0) for k in range(KD)] + [(("gate", 0), 0), (("softmax", 0), 0)])


def filler_at(step, feeds, leads):
    name, piece = FILLERS[step]
    if name is None or not (leads if name[0] == "next" else feeds):
        return None, 0
    return name, piece


def opening(attends, feeds):
    strips = [[(w, g) for w in ("qs", "ks")] for g in range(HC)]
    qk = [("q", 0), ("k", 0), ("q", 1), ("k", 1)]
    order = [] if feeds else [("cond", o) for o in range(KD)]
    for n in range(2 * KD):
        order += [("fold_i", n), qk[n]]
    dense = [("v", 0), ("v", 1), ("x1t", 0), ("x1t", 1)]
    for n, ready in enumerate([[], strips[0], strips[1], strips[2] + strips[3]]):
        order += [dense[n], ("fold_o", n)] + ready
    for j in range(HID_EARLY):
        order += [("hid", j)] + strips[4 + j]
    ours = ("cond", "q", "k", "v", "qs", "ks")
    return [n for n in order if (attends if n[0] in ours else feeds)]


def psum_plan(attends, feeds, leads):
    rings = {"linear": [0, 1, 2, 3, 7], "score": [0, 1, 2], "filler": [3, 7], "t": [4, 5],
             "pv": [PV_BANK]}
    if not attends:
        rings["filler"] = rings["linear"]
    turn = dict.fromkeys(rings, 0)
    uses = [0] * 8
    plan = {}

    def take(name, kind):
        bank = rings[kind][turn[kind] % len(rings[kind])]
        turn[kind] += 1
        plan[name] = (bank, uses[bank])
        uses[bank] += 1

    for name in opening(attends, feeds):
        take(name, "linear")
    for step in range(STEPS):
        ss, ts, pvs, _, rt, _ = units_at(step) if attends else ((), (), (), None, None, None)
        for s in ss:
            take(("s", s), "score")
        for t in ts:
            take(("t", t), "t")
        if rt is not None:
            take(("rt", rt), "score")
        name, piece = filler_at(step, feeds, leads)
        if name is not None and piece == 0 and name[0] != "softmax":
            take(name, "filler")
        for pv in pvs:
            if pv % HEADS == 0:
                take(("pv", pv // HEADS), "pv")
    return plan, uses


assert len(FILLERS) == STEPS


class Round:
    first_plan, first_uses = psum_plan(True, False, True)
    full_plan, full_uses = psum_plan(True, True, True)
    end_plan, end_uses = psum_plan(True, True, False)
    last_plan, last_uses = psum_plan(False, True, False)

    def __init__(self, b):
        first, end, last = (isinstance(b, int) and b == i for i in (0, B - 1, B))
        self.n = b
        self.b = None if last else b
        self.p = None if first else b - 1
        self.leads = not end and not last
        self.plan = (Round.first_plan if first else Round.end_plan if end else Round.last_plan if last
                     else Round.full_plan)
        self.opening = opening(not last, not first)

    def filler(self, step):
        return filler_at(step, self.p is not None, self.leads)

    def start(self, i, more=0):
        if isinstance(self.n, int) and self.n == 0:
            return more
        if isinstance(self.n, int) and self.n == B:
            return Round.total(i) - Round.last_uses[i] + more
        return self.n * Round.full_uses[i] + (Round.first_uses[i] - Round.full_uses[i] + more)

    @staticmethod
    def total(i):
        return Round.first_uses[i] + (B - 2) * Round.full_uses[i] + Round.end_uses[i] + Round.last_uses[i]


def build_kernel(nc, xT, x_cond_w, x_cond_b, itok, wq, wk, wv, wo, wi_t, wo_t, lora_c, lora_e,
                 gate_w, gate_b, w1, w2, w3, b1, b2, b3, ident, maskd, tri, sel, iota_r, iota_t,
                 tok, thr, out):
    hrows = nc.dram_tensor("hrows", [B * S, ROW], F32, kind="Internal").ap()
    out_rows = out.rearrange("b s d -> (b s) d")

    outer = ExitStack()
    part_a = ExitStack()
    with outer:
        def sb(name, shape, dt, ctx=outer):
            return ctx.enter_context(nc.sbuf_tensor(name, shape, dt))

        def sem(name):
            return outer.enter_context(nc.semaphore(name))

        bank = [outer.enter_context(nc.psum_tensor(f"bank{i}", [P, 512], F32)) for i in range(8)]

        id_f = sb("id_f", [P, P], F32)
        id_b = sb("id_b", [P, P], BF16)
        mask_b = sb("mask_b", [P, P], BF16)
        mask_f = sb("mask_f", [P, P], F32)
        itok_sb = sb("itok_sb", [1, B], I32)
        gb_sb = sb("gb_sb", [P, NE], F32)
        logits = sb("logits", [P, NT, NE], F32)
        tri_f = sb("tri_f", [P, P], F32)
        iota_r_sb = sb("iota_r_sb", [P, P], F32)
        iota_t_sb = sb("iota_t_sb", [P, TW], F32)
        tok_sb = sb("tok_sb", [P, NT], F32)
        thr_sb = sb("thr_sb", [P, 2 * NT + NE], F32)

        attn = ExitStack()
        with attn:
            q_sb = sb("q_sb", [P, HC, S], F32R, attn)
            k_sb = sb("k_sb", [P, HC, S], F32R, attn)
            v_sb = sb("v_sb", [P, TB, HEADS // 2, 2, 2, DH], F32, attn)
            probs = sb("probs", [P, 4, S], F32, attn)
            probs_t = sb("probs_t", [P, 4, S], F32, attn)
            x_in = sb("x_in", [P, KD, S], F32, attn)
            cond = sb("cond", [P, KD, S], F32, attn)
        w2_sb = sb("w2_sb", [P, NE, KH, H], F32)

        x_res = sb("x_res", [P, KD, S], F32, part_a)
        wc_sb = sb("wc_sb", [P, KD, D], F32, part_a)
        bc_sb = sb("bc_sb", [P, KD], F32, part_a)
        wq_raw = sb("wq_raw", [P, KD, D], F32, part_a)
        wk_sb = sb("wk_sb", [P, KD, D], F32, part_a)
        wv_sb = sb("wv_sb", [P, KD, D], F32, part_a)
        wo_sb = sb("wo_sb", [P, KD, D], F32, part_a)
        sel_sb = sb("sel_sb", [P, 4, 4, P], F32R, part_a)
        nmax = sb("nmax", [P, 8], F32, part_a)
        rsum = sb("rsum", [P, 2, HEADS], F32, part_a)
        rinv = sb("rinv", [P, HEADS], F32, part_a)
        rrep = sb("rrep", [P, D], F32, part_a)
        rt_sb = sb("rt_sb", [P, D], F32, part_a)
        ot_sb = sb("ot_sb", [P, KD, S], F32, part_a)
        x_high = sb("x_high", [P, KD, S], F32R, part_a)
        x_low = sb("x_low", [P, KD, S], F32R, part_a)
        wi_base = sb("wi_base", [P, KD, F], F32, part_a)
        wi_high = sb("wi_high", [P, KD, F], F32R, part_a)
        wi_low = sb("wi_low", [P, KD, F], F32R, part_a)
        wf_base = sb("wf_base", [P, KF, D], F32, part_a)
        wf_high = sb("wf_high", [P, KF, D], F32R, part_a)
        wf_low = sb("wf_low", [P, KF, D], F32R, part_a)
        lora = sb("lora", [4 * R, D + F], F32, part_a)
        with ExitStack() as shared:
            parts = sb("parts", [P, KD, 4, S], F32R, shared)
        hid_high = sb("hid_high", [P, KF, S], F32R, part_a)
        with ExitStack() as shared:
            sel_f = sb("sel_f", [P, 4, 4, P], F32, shared)
        hid_low = sb("hid_low", [P, KF, S], F32R, part_a)
        x1_sb = sb("x1_sb", [P, TB, D], F32, part_a)
        h_sb = sb("h_sb", [P, TB, ROW], F32, part_a)
        with ExitStack() as shared:
            x1t = sb("x1t", [P, KD, S], F32, shared)
        ht_sb = sb("ht_sb", [P, KD, S], F32, part_a)
        gw_sb = sb("gw_sb", [P, KD, NE], F32, part_a)
        glog = sb("glog", [P, TB, NE], F32, part_a)
        gmax = sb("gmax", [P, TB], F32, part_a)
        gexp = sb("gexp", [P, TB, NE], F32, part_a)
        gsum = sb("gsum", [P, TB], F32, part_a)
        ginv = sb("ginv", [P, TB], F32, part_a)
        part_a.close()

        etab = sb("etab", [1, TILES, AHEAD], I32)
        gather_id = sb("gather_id", [P, TILES], U32)
        scatter_id = sb("scatter_id", [P, TILES], U32)
        with ExitStack() as route:
            tri_sb = sb("tri_sb", [P, P], BF16, route)
            ones_b = sb("ones_b", [P, P], BF16, route)
            m1 = sb("m1", [P, NT], F32, route)
            rk = sb("rk", [P, NT, NE], F32, route)
            lg2 = sb("lg2", [P, NT, NE], F32, route)
            hot = [sb(f"hot{c}", [P, NT, NE], F32, route) for c in range(2)]
            hots = sb("hots", [P, NT, NE], BF16, route)
            pre = sb("pre", [P, NT, NE], F32, route)
            cmpt = sb("cmpt", [P, NE, NT * 2], F32, route)
            ntile = sb("ntile", [P, NE], F32, route)
            tbase = sb("tbase", [P, NE + 1], F32, route)
            slot = sb("slot", [P, NT], F32, route)
            s_r = sb("s_r", [P, 2, NT], F32, route)
            s_j = sb("s_j", [P, 2, NT], F32, route)
            s_i = sb("s_i", [P, 2, NT], I32, route)
            hit_r = sb("hit_r", [P, 2, HIT_GROUP, P], F32R, route)
            hit_j = sb("hit_j", [P, 2, HIT_GROUP, TW], F32, route)
            hit_v = sb("hit_v", [P, 2, HIT_GROUP, TW], F32R, route)
            ids_f = sb("ids_f", [P, TILES], F32, route)
            ids_g = sb("ids_g", [P, TILES], F32, route)
            starts = sb("starts", [1, TILES, NE - 1], F32, route)
            expert_f = sb("expert_f", [1, TILES], F32, route)
        xg = sb("xg", [P, ROW], F32)
        xgt = sb("xgt", [P, KD, P], F32)
        gid = sb("gid", [P, 1], U32)
        sid = sb("sid", [P, 1], U32)
        wsel = sb("wsel", [P, TILES], F32)
        z1 = sb("z1", [P, H], F32)
        z2 = sb("z2", [P, H], F32)
        g1 = sb("g1", [P, H], F32)
        g2 = sb("g2", [P, H], F32)
        g1t = sb("g1t", [P, KH, P], F32)
        g2t = sb("g2t", [P, KH, P], F32)
        y0 = sb("y0", [P, D], F32)
        y_sb = sb("y_sb", [P, D], F32)
        behind_route = sb("behind_route", [P, ROUTE_REST], F32)
        w1_sb = sb("w1_sb", [P, NE, KD, H], F32)
        w3_sb = sb("w3_sb", [P, NE, KH, D], F32)
        b1_sb = sb("b1_sb", [P, NE, H], F32)
        b2_sb = sb("b2_sb", [P, NE, H], F32)
        b3_sb = sb("b3_sb", [P, NE, D], F32)

        full = [sem(f"bank{i}_filled") for i in range(8)]
        free = [sem(f"bank{i}_drained") for i in range(8)]
        s_itok = sem("s_itok")
        s_const = sem("s_const")
        s_sel_f = sem("s_sel_f")
        s_sel = sem("s_sel")
        s_mid = sem("s_mid")
        s_x_high = sem("s_x_high")
        s_x_low = sem("s_x_low")
        s_eff = sem("s_eff")
        s_eff_high = sem("s_eff_high")
        s_hid_high = sem("s_hid_high")
        s_in = sem("s_in")
        s_xres = sem("s_xres")
        s_lora = sem("s_lora")
        s_x1out = sem("s_x1out")
        s_hout = sem("s_hout")
        s_prep = sem("s_prep")
        s_idb = sem("s_idb")
        s_hi = sem("s_hi")
        s_max = sem("s_max")
        s_chain = sem("s_chain")
        s_rrep = sem("s_rrep")
        s_vzero = sem("s_vzero")
        s_gneg = sem("s_gneg")
        s_gexp = sem("s_gexp")
        s_gchain = sem("s_gchain")
        s_hdone = sem("s_hdone")
        s_rchain = sem("s_rchain")
        s_rconst = sem("s_rconst")
        s_ohot = sem("s_ohot")
        s_cnts = sem("s_cnts")
        s_hit_r = sem("s_hit_r")
        s_hit_j = sem("s_hit_j")
        s_hit_v = sem("s_hit_v")
        s_hitu = sem("s_hitu")
        s_route = sem("s_route")
        s_w1 = sem("s_w1")
        s_w2 = sem("s_w2")
        s_w3 = sem("s_w3")
        s_bias = sem("s_bias")
        s_gid = sem("s_gid")
        s_xg = sem("s_xg")
        s_wsel = sem("s_wsel")
        s_z1 = sem("s_z1")
        s_g1 = sem("s_g1")
        s_z2 = sem("s_z2")
        s_g2 = sem("s_g2")
        s_y = sem("s_y")
        s_sid = sem("s_sid")
        s_tick = sem("s_tick")
        s_add = sem("s_add")
        N_CONST, N_MID, N_RC = 5, 7, 5
        BX, BT1, BT2, BL1, BL2, BL3 = 0, 1, 2, 3, 4, 5

        block = outer.enter_context(nc.Block())

        def filled(eng, name, rd):
            i, k = rd.plan[name]
            eng.wait_ge(full[i], rd.start(i, k + 1))

        def drained(eng, name, rd):
            i, k = rd.plan[name]
            eng.wait_ge(free[i], rd.start(i, k + 2))

        def vacant(eng, name, rd, after=()):
            least = {rd.plan[name][0]: rd.plan[name][1] + 1}
            for other in after:
                i, k = rd.plan[other]
                least[i] = max(least.get(i, 0), k + 2)
            for i, v in least.items():
                eng.wait_ge(free[i], rd.start(i, v))

        def at(name, rd):
            return bank[rd.plan[name][0]]

        def done(ins, name, rd):
            ins.then_inc(full[rd.plan[name][0]], 1)

        def taken(ins, name, rd):
            ins.then_inc(free[rd.plan[name][0]], 1)

        FOLDS = 2 * KD + KF // 2

        def fold_index(n):
            return n[1] + (2 * KD if n[0] == "fold_o" else 0)

        def on_act(t):
            return t % 4 == 3 or (t % 2 == 1 and t >= 2 * HEADS)

        before_b = [Round.total(i) for i in range(8)]
        PRE_BANK, ID_BANK = 0, 1
        LEAD_BANKS = (3, 7)
        b_uses = [1, 1] + [0] * (8 - 2)
        before_c = [before_b[i] + b_uses[i] for i in range(8)]

        @block.sync
        def _(sp):
            sp.dma_start(itok_sb[:, :], itok).then_inc(s_itok, 16)
            sp.dma_start(wq_raw[:, :, :], wq).then_inc(s_const, 16)
            sp.wait_ge(s_itok, 16)

            def expert_of(b):
                return sp.value_load(itok_sb[0:1, bass.ds(b, 1)], min_val=0, max_val=NE - 1)

            def load_in(b, e):
                sp.dma_start(x_in[:, :, :], xT[bass.ds(b, 1), :, :, :].rearrange("o p k t -> (o p) k t")
                             ).then_inc(s_in, 16)
                sp.dma_start(wc_sb[:, :, :], x_cond_w[bass.ds(e, 1), :, :, :].rearrange("o p k t -> (o p) k t")
                             ).then_inc(s_in, 16)
                sp.dma_start(bc_sb[:, :], x_cond_b[bass.ds(e, 1), :, :].rearrange("o p k -> (o p) k")
                             ).then_inc(s_in, 16)

            def load_lora(e):
                for r, c in ((R, 0), (3 * R, D + F)):
                    sp.dma_start(lora[r:r + R, :], lora_e[bass.ds(e, 1), :, c:c + D + F].rearrange("o r n -> (o r) n")
                                 ).then_inc(s_lora, 16)

            def load_res(b):
                sp.dma_start(x_res[:, :, :], xT[bass.ds(b, 1), :, :, :].rearrange("o p k t -> (o p) k t")
                             ).then_inc(s_xres, 16)

            def value(rd, name, more):
                i, k = rd.plan[name]
                v = rd.start(i, k + more)
                return v if isinstance(v, int) else sp.snap(v)

            def wait_for(rd, sems, names, values):
                for name, v in zip(names, values):
                    sp.wait_ge(sems[rd.plan[name][0]], v)
                    sp.sem_inc(s_tick, 1)

            conds = [("cond", o) for o in range(KD)]
            x1ts = [("x1t", o) for o in range(KD)]
            folds = [("fold_o", KF // 2 - 1)]
            x1s = [("x1", t2) for t2 in range(TB // 2)]

            def turn(rd, last=False):
                if rd.b is not None:
                    if not last:
                        b1_ = rd.b + 1 if isinstance(rd.b, int) else sp.snap(rd.b + 1)
                        e_next = expert_of(b1_)
                        if rd.p is None:
                            v_read = value(rd, conds[-1], 1)
                            v_cond = [value(rd, n, 2) for n in conds]
                        else:
                            v_led = [(i, sp.snap(rd.start(i)), sp.snap(rd.start(i, 1))) for i in LEAD_BANKS]
                    if rd.p is not None:
                        e = expert_of(rd.b)
                if rd.p is not None:
                    p = rd.p if isinstance(rd.p, int) else sp.snap(rd.p)
                    v_hdone = rd.p + 1 if isinstance(rd.p, int) else rd.b
                    v_x1t = [value(rd, n, 2) for n in x1ts]
                    v_fold = [value(rd, n, 1) for n in folds]
                    v_x1 = [value(rd, n, 2) for n in x1s]
                if rd.b is not None and not last:
                    if rd.p is None:
                        wait_for(rd, full, conds[-1:], [v_read])
                        wait_for(rd, free, conds, v_cond)
                    else:
                        for i, v_full, v_free in v_led:
                            sp.wait_ge(full[i], v_full)
                            sp.sem_inc(s_tick, 1)
                            sp.wait_ge(free[i], v_free)
                            sp.sem_inc(s_tick, 1)
                    load_in(b1_, e_next)
                if rd.p is not None:
                    if rd.b is not None:
                        wait_for(rd, free, x1ts, v_x1t)
                        load_res(rd.b)
                        wait_for(rd, full, folds, v_fold)
                        load_lora(e)
                    wait_for(rd, free, x1s, v_x1)
                    sp.dma_start(out[bass.ds(p, 1), :, :].rearrange("o (t p) d -> p (o t) d", p=P),
                                 x1_sb[:, :, :]).then_inc(s_x1out, 16)
                    sp.wait_ge(s_hdone, v_hdone)
                    sp.sem_inc(s_tick, 1)
                    sp.dma_start(hrows[bass.ds(p * S, S), :].rearrange("(t p) d -> p t d", p=P),
                                 h_sb[:, :, :]).then_inc(s_hout, 16)

            e0 = expert_of(0)
            load_in(0, e0)
            sp.dma_start(wk_sb[:, :, :], wk).then_inc(s_const, 16)
            sp.dma_start(wv_sb[:, :, :], wv).then_inc(s_const, 16)
            sp.dma_start(id_f[:, :], ident).then_inc(s_const, 16)
            sp.dma_start(mask_f[:, :], maskd).then_inc(s_const, 16)
            sp.dma_start(sel_f[:, :, :, :], sel).then_inc(s_sel_f, 16)
            sp.dma_start(wo_sb[:, :, :], wo).then_inc(s_mid, 16)
            sp.dma_start(lora[0:R, :], lora_c[:, 0:D + F]).then_inc(s_mid, 16)
            sp.dma_start(lora[2 * R:3 * R, :], lora_c[:, D + F:LORA]).then_inc(s_mid, 16)
            load_lora(e0)
            load_res(0)
            sp.dma_start(wi_base[:, :, :], wi_t).then_inc(s_mid, 16)
            sp.dma_start(wf_base[:, :, :], wo_t).then_inc(s_mid, 16)
            sp.dma_start(gw_sb[:, :, :], gate_w).then_inc(s_mid, 16)
            sp.dma_start(gb_sb[:, :], gate_b.partition_broadcast(P)).then_inc(s_mid, 16)
            turn(Round(0))
            with sp.Fori(1, B - 1) as b:
                turn(Round(b))
            turn(Round(B - 1), last=True)
            sp.dma_start(tri_f[:, :], tri).then_inc(s_rconst, 16)
            sp.dma_start(iota_r_sb[:, :], iota_r).then_inc(s_rconst, 16)
            sp.dma_start(iota_t_sb[:, :], iota_t).then_inc(s_rconst, 16)
            sp.dma_start(tok_sb[:, :], tok).then_inc(s_rconst, 16)
            sp.dma_start(thr_sb[:, :], thr).then_inc(s_rconst, 16)
            for i in range(8):
                sp.wait_ge(full[i], Round(B).start(i))
                sp.wait_ge(free[i], Round(B).start(i) + 1)
            for e in range(NE):
                sp.dma_start(w2_sb[:, e, :, :], w2[e]).then_inc(s_w2, 16)
            turn(Round(B))
            sp.wait_ge(s_x1out, 16 * B + 1)
            sp.wait_ge(s_hout, 16 * B + 1)
            for i in range(8):
                sp.wait_ge(full[i], before_b[i])
                sp.wait_ge(free[i], before_b[i] + 1)
            for e in range(NE):
                sp.dma_start(w1_sb[:, e, :, :], w1[e]).then_inc(s_w1, 16)
            sp.dma_start(b1_sb[:, :, :].rearrange("p e d -> p (e d)"), b1.partition_broadcast(P)).then_inc(s_bias, 16)
            sp.dma_start(b2_sb[:, :, :].rearrange("p e d -> p (e d)"), b2.partition_broadcast(P)).then_inc(s_bias, 16)
            sp.dma_start(b3_sb[:, :, :].rearrange("p e d -> p (e d)"), b3.partition_broadcast(P)).then_inc(s_bias, 16)
            for e in range(NE):
                sp.dma_start(w3_sb[:, e, :, :], w3[e]).then_inc(s_w3, 16)
            sp.wait_ge(s_add, 16 * TILES)

        @block.tensor
        def _(pe):
            for i in range(8):
                pe.sem_inc(free[i], 1)

            def mm(*a, **k):
                return nc.tensor.matmul(*a, **k)

            def product(rd, n, piece=None):
                what, m = n
                if what == "softmax":
                    return
                b, p = rd.b, rd.p

                def dst():
                    return at(n, rd)

                if what in ("cond", "next"):
                    if piece in (None, 0):
                        if m == 0:
                            pe.wait_ge(s_in, b * 48 + (48 if what == "cond" else 96))
                        vacant(pe, n, rd)
                    for k in range(KD) if piece is None else (piece,):
                        ins = mm(dst()[:, :], wc_sb[:, k, m * P:(m + 1) * P], x_in[:, k, :],
                                 start=(k == 0), stop=(k == KD - 1))
                    if piece not in (None, KD - 1):
                        return
                elif what in ("q", "k"):
                    if n == ("q", 0) and p is not None:
                        for i in LEAD_BANKS:
                            pe.wait_ge(free[i], rd.start(i, 1))
                    vacant(pe, n, rd, [("cond", o) for o in range(KD)] if n == ("q", 0) and p is None else ())
                    w = wq_raw if what == "q" else wk_sb
                    for k in range(KD):
                        ins = mm(dst()[:, :], w[:, k, m * P:(m + 1) * P], cond[:, k, :],
                                 start=(k == 0), stop=(k == KD - 1))
                elif what == "v":
                    vacant(pe, n, rd)
                    for u in range(2):
                        t = 2 * m + u
                        for k in range(KD):
                            ins = mm(dst()[:, u * D:(u + 1) * D], cond[:, k, t * P:(t + 1) * P], wv_sb[:, k, :],
                                     start=(k == 0), stop=(k == KD - 1))
                elif what in ("qs", "ks"):
                    c, pair = divmod(m, 4)
                    slot = 0 if what == "qs" else 2
                    vacant(pe, n, rd, [(what[0], c)])
                    for u in range(2):
                        ins = mm(dst()[:, :], sel_sb[:, slot + u, pair, :], parts[:, c, slot + u, :],
                                 start=(u == 0), stop=(u == 1))
                elif what == "fold_i":
                    if m == 0:
                        pe.wait_ge(s_lora, p * 32 + 32)
                    k, fh = m // 2, m % 2
                    vacant(pe, n, rd)
                    ins = mm(dst()[:, :], lora[0:2 * R, k * P:(k + 1) * P], lora[0:2 * R, D + fh * 512:D + (fh + 1) * 512],
                             start=True, stop=True)
                elif what == "fold_o":
                    vacant(pe, n, rd)
                    for u in range(2):
                        j = 2 * m + u
                        ins = mm(dst()[:, u * D:(u + 1) * D], lora[2 * R:4 * R, j * P:(j + 1) * P],
                                 lora[2 * R:4 * R, F:F + D], start=True, stop=True)
                elif what == "x1t":
                    if m == 0:
                        pe.wait_ge(free[PV_BANK], rd.start(PV_BANK, 1))
                    vacant(pe, n, rd)
                    for k in range(KD):
                        ins = mm(dst()[:, :], wo_sb[:, k, m * P:(m + 1) * P], ot_sb[:, k, :],
                                 start=(k == 0), stop=(k == KD - 1))
                elif what == "hid":
                    if piece in (None, 0):
                        vacant(pe, n, rd, ([("fold_i", n4) for n4 in range(2 * KD)] +
                                           [("x1t", o) for o in range(KD)]) if m == 0 else ())
                    if m == 0:
                        pe.wait_ge(s_x_low, p * KD + KD)
                    for k in range(KD) if piece is None else (piece,):
                        cols = slice(m * P, (m + 1) * P)
                        for w, x in ((wi_high, x_high), (wi_high, x_low), (wi_low, x_high)):
                            ins = mm(dst()[:, :], w[:, k, cols], x[:, k, :], start=(k == 0 and w is wi_high and x is x_high),
                                     stop=(k == KD - 1 and w is wi_low))
                    if piece not in (None, KD - 1):
                        return
                elif what == "h":
                    if piece == 0:
                        vacant(pe, n, rd, ([("fold_o", n4) for n4 in range(KF // 2)] +
                                           [("hid", j) for j in range(KF)]) if m == 0 else ())
                    per = KF // H_PIECES
                    for j in range(per * piece, per * (piece + 1)):
                        rows = slice(m * P, (m + 1) * P)
                        for g, w in ((hid_high, wf_high), (hid_high, wf_low), (hid_low, wf_high)):
                            ins = mm(dst()[:, 0:D], g[:, j, rows], w[:, j, :],
                                     start=(j == 0 and g is hid_high and w is wf_high),
                                     stop=(j == KF - 1 and g is hid_low))
                    if piece < H_PIECES - 1:
                        return
                elif what == "ht":
                    vacant(pe, n, rd, [("h", t) for t in range(TB)] if m == 0 else ())
                    for t in range(TB):
                        ins = nc.tensor.transpose(dst()[:, t * P:(t + 1) * P], h_sb[:, t, m * P:(m + 1) * P],
                                                  id_f[:, :])
                elif what == "gate":
                    vacant(pe, n, rd, [("ht", k) for k in range(KD)])
                    for t in range(TB):
                        for k in range(KD):
                            ins = mm(dst()[:, t * NE:(t + 1) * NE], ht_sb[:, k, t * P:(t + 1) * P],
                                     gw_sb[:, k, :], start=(k == 0), stop=(k == KD - 1))
                else:
                    vacant(pe, n, rd)
                    for u in range(2):
                        t = 2 * m + u
                        for k in range(KD):
                            ins = nc.tensor.transpose(dst()[:, u * D + k * P:u * D + (k + 1) * P],
                                                      x1t[:, k, t * P:(t + 1) * P], id_f[:, :])
                done(ins, n, rd)

            def turn(rd):
                b, p = rd.b, rd.p
                for n in rd.opening:
                    if p is None and n == ("q", 0):
                        pe.wait_ge(s_const, 16 * N_CONST)
                        pe.wait_ge(s_idb, 1)
                        pe.wait_ge(s_prep, 1)
                    if p is None and n == ("qs", 0):
                        pe.wait_ge(s_sel, 1)
                    product(rd, n)
                values = [("v", t2) for t2 in range(TB // 2)] + [(w, g) for g in range(HC) for w in ("qs", "ks")]
                for step in range(STEPS):
                    n_fill, piece = rd.filler(step)
                    if b is None:
                        if n_fill is not None:
                            product(rd, n_fill, piece)
                        continue
                    ss, ts, pvs, _, rt, _ = units_at(step)
                    for s in ss:
                        w = (s // HEADS + 1) * P
                        vacant(pe, ("s", s), rd, values if s == 0 else ())
                        mm(at(("s", s), rd)[:, w - P:w], id_b[:, :], mask_b[:, :], start=True, stop=False,
                           skip_group_check=True)
                    for s in ss:
                        i, h = divmod(s, HEADS)
                        g, r = h // 2, STRIP * (h % 2)
                        n = ("s", s)
                        w = (i + 1) * P
                        done(mm(at(n, rd)[:, 0:w], q_sb[r:r + STRIP, g, i * P:(i + 1) * P],
                                k_sb[r:r + STRIP, g, 0:w], start=False, stop=True,
                                skip_group_check=True), n, rd)
                    for t in ts:
                        n = ("t", t)
                        vacant(pe, n, rd, [("s", t)])
                        for kb in range(t // HEADS + 1):
                            ins = nc.tensor.transpose(at(n, rd)[:, kb * P:(kb + 1) * P],
                                                      probs[:, t % 4, kb * P:(kb + 1) * P], id_f[:, :])
                        done(ins, n, rd)
                    if rt is not None:
                        n = ("rt", rt)
                        pe.wait_ge(s_rrep, b * TB + (rt + 1))
                        vacant(pe, n, rd)
                        for k in range(KD):
                            ins = nc.tensor.transpose(at(n, rd)[:, k * P:(k + 1) * P],
                                                      rrep[:, k * P:(k + 1) * P], id_f[:, :])
                        done(ins, n, rd)
                    if n_fill is not None:
                        product(rd, n_fill, piece)
                    for pv in pvs:
                        i, h = divmod(pv, HEADS)
                        n = ("pv", i)
                        if h == 0:
                            vacant(pe, n, rd, [("t", pv)])
                        else:
                            drained(pe, ("t", pv), rd)
                        r, col = PART * (h % 8 // 2), P * (h // 8)
                        for kb in range(i + 1):
                            ins = mm(at(n, rd)[r:r + PART, col:col + P],
                                     v_sb[:, kb, h // 2, h % 2, :, :].rearrange("p a d -> p (a d)"),
                                     probs_t[:, pv % 4, kb * P:(kb + 1) * P],
                                     start=(h % 2 == 0 and kb == 0), stop=(h % 2 == 1 and kb == i))
                        if h == HEADS - 1:
                            done(ins, n, rd)

            turn(Round(0))
            pe.wait_ge(s_mid, 16 * N_MID)
            with pe.Fori(1, B - 1) as b:
                turn(Round(b))
            turn(Round(B - 1))
            turn(Round(B))

            pe.wait_ge(s_ohot, 1)
            pe.wait_ge(s_rconst, 16 * N_RC)
            pe.wait_ge(free[PRE_BANK], before_b[PRE_BANK] + 1)
            mm(bank[PRE_BANK][:, 0:NT * NE], tri_sb[:, :], hots[:, :, :].rearrange("p t e -> p (t e)"),
               start=True, stop=False, skip_group_check=True)
            for t in range(NT):
                later = NT - t
                ins = mm(bank[PRE_BANK][:, (t + 1) * NE:(NT + 1) * NE].rearrange("p (t e) -> p t e", e=NE),
                         ones_b[:, :], hots[:, t, :].unsqueeze(1).to_broadcast([P, later, NE]),
                         start=False, stop=(t == NT - 1), skip_group_check=True)
            ins.then_inc(full[PRE_BANK], 1)
            pe.wait_ge(free[ID_BANK], before_b[ID_BANK] + 1)
            for n in range(2 * NT // HIT_GROUP):
                pe.wait_ge(s_hit_r, n + 1)
                pe.wait_ge(s_hit_v, n + 1)
                for t in range(HIT_GROUP):
                    ins = mm(bank[ID_BANK][:, 0:TW], hit_r[:, n % 2, t, :], hit_v[:, n % 2, t, :],
                             start=(n == 0 and t == 0), stop=(n == 2 * NT // HIT_GROUP - 1 and t == HIT_GROUP - 1))
                ins.then_inc(s_hitu, 1)
            pe.wait_ge(s_route, 1)
            pe.wait_ge(s_w1, 16 * NE)

            e_regs = [pe.alloc_register(f"pe_expert{d}") for d in range(AHEAD)]

            def experts(j):
                pe.load(e_regs, etab[0:1, bass.ds(max(j, 0), 1) if isinstance(j, int) else bass.ds(j, 1), :]
                         .rearrange("p o d -> p (o d)"))
                e = [pe.snap(reg, min_val=0, max_val=NE - 1) for reg in e_regs]
                return [None] * -j + e if isinstance(j, int) and j < 0 else e

            def up(i, j):
                return before_c[i] + 1 + j

            def x_trans(j):
                pe.wait_ge(s_xg, 16 * j + 16)
                pe.wait_ge(free[BX], up(BX, j))
                for k in range(KD):
                    ins = nc.tensor.transpose(bank[BX][:, k * P:(k + 1) * P], xg[:, k * P:(k + 1) * P], id_f[:, :])
                ins.then_inc(full[BX], 1)

            def layer1(j, e):
                pe.wait_ge(free[BX], up(BX, j) + 1)
                for k in range(KD):
                    ins = mm(bank[BL1][:, :], xgt[:, k, :],
                             w1_sb[:, bass.ds(e, 1), k, :].rearrange("p o n -> p (o n)"),
                             start=(k == 0), stop=(k == KD - 1))
                ins.then_inc(full[BL1], 1)

            def g_trans(j, g, s_g, bt):
                pe.wait_ge(s_g, j + 1)
                pe.wait_ge(free[bt], up(bt, j))
                for k in range(KH):
                    ins = nc.tensor.transpose(bank[bt][:, k * P:(k + 1) * P], g[:, k * P:(k + 1) * P], id_f[:, :])
                ins.then_inc(full[bt], 1)

            def layer2(j, e, half):
                if half == 0:
                    pe.wait_ge(free[BT1], up(BT1, j) + 1)
                for k in range(2 * half, 2 * half + 2):
                    ins = mm(bank[BL2][:, :], g1t[:, k, :],
                             w2_sb[:, bass.ds(e, 1), k, :].rearrange("p o n -> p (o n)"),
                             start=(k == 0), stop=(k == KH - 1))
                if half == 1:
                    ins.then_inc(full[BL2], 1)

            def layer3(j, e):
                pe.wait_ge(free[BT2], up(BT2, j) + 1)
                pe.wait_ge(free[BL3], up(BL3, j))
                for k in range(KH):
                    ins = mm(bank[BL3][:, 0:D], g2t[:, k, :],
                             w3_sb[:, bass.ds(e, 1), k, :].rearrange("p o n -> p (o n)"),
                             start=(k == 0), stop=(k == KH - 1))
                ins.then_inc(full[BL3], 1)

            def step(j, has):
                e = experts(j)
                if has(2):
                    layer1(j + 2, e[2])
                if has(0):
                    g_trans(j, g2, s_g2, BT2)
                if has(1):
                    layer2(j + 1, e[1], 0)
                if has(0):
                    layer3(j, e[0])
                if has(3):
                    x_trans(j + 3)
                if has(1):
                    layer2(j + 1, e[1], 1)
                if has(2):
                    g_trans(j + 2, g1, s_g1, BT1)

            for j in (-3, -2):
                step(j, lambda d: 0 <= j + d)
            pe.wait_ge(s_w2, 16 * NE)
            pe.wait_ge(s_w3, 16 * NE)
            step(-1, lambda d: -1 + d >= 0)
            with pe.Fori(0, TILES - 3) as j:
                step(j, lambda d: True)
            for j in range(TILES - 3, TILES):
                step(j, lambda d: j + d < TILES)

        @block.scalar
        def _(act):
            act.sem_inc(s_x1out, 1)

            def take(rd, n, piece=None):
                what, m = n
                b, p = rd.b, rd.p
                if what == "cond" or what == "next" and piece == KD - 1:
                    if m == 0:
                        act.wait_ge(s_in, b * 48 + (48 if what == "cond" else 96))
                    filled(act, n, rd)
                    ins = nc.scalar.activation(cond[:, m, :], at(n, rd)[:, :], ACT.Identity, bias=bc_sb[:, m:m + 1])
                elif what in ("q", "k"):
                    filled(act, n, rd)
                    nc.scalar.copy(parts[:, m, 0 if what == "q" else 2, :], at(n, rd)[:, :]).then_inc(s_hi, 1)
                    return
                elif what == "v":
                    filled(act, n, rd)
                    v_ps = at(n, rd)[:, :].rearrange("p (t s e d) -> p t s e d", t=2, e=2, d=DH)
                    nc.scalar.copy(v_sb[:, 2 * m:2 * m + 2, :, 0, 0, :], v_ps[:, :, :, 0, :])
                    ins = nc.scalar.copy(v_sb[:, 2 * m:2 * m + 2, :, 1, 1, :], v_ps[:, :, :, 1, :])
                elif what == "qs":
                    filled(act, n, rd)
                    ins = nc.scalar.copy(q_sb[:, m, :], at(n, rd)[:, :])
                elif what == "x1t":
                    drained(act, n, rd)
                    nc.scalar.copy(x_high[:, m, :], x1t[:, m, :]).then_inc(s_x_high, 1)
                    return
                elif what in ("fold_i", "fold_o"):
                    act.wait_ge(s_eff, p * FOLDS + (fold_index(n) + 1))
                    if what == "fold_i":
                        dst = wi_high[:, m // 2, m % 2 * 512:(m % 2 + 1) * 512]
                    else:
                        dst = wf_high[:, 2 * m:2 * m + 2, :].rearrange("p j d -> p (j d)")
                    nc.scalar.copy(dst, at(n, rd)[:, :]).then_inc(s_eff_high, 1)
                    return
                elif what == "hid" and piece in (None, KD - 1):
                    filled(act, n, rd)
                    nc.scalar.activation(hid_high[:, m, :], at(n, rd)[:, :], ACT.Relu).then_inc(s_hid_high, 1)
                    return
                elif what == "ht" and m == 1:
                    filled(act, n, rd)
                    ins = nc.scalar.copy(ht_sb[:, 1, :], at(n, rd)[:, :])
                elif what == "gate":
                    act.wait_ge(s_gneg, p + 1)
                    nc.scalar.activation(gexp[:, :, :], gexp[:, :, :], ACT.Exp).then_inc(s_gexp, 1)
                    return
                elif what == "x1":
                    if m == 0:
                        act.wait_ge(s_x1out, p * 16 + 1)
                    filled(act, n, rd)
                    ins = nc.scalar.copy(x1_sb[:, 2 * m:2 * m + 2, :].rearrange("p t d -> p (t d)"), at(n, rd)[:, :])
                else:
                    return
                taken(ins, n, rd)

            def turn(rd):
                b, p = rd.b, rd.p
                for n in rd.opening:
                    if p is None and n == ("q", 0):
                        act.wait_ge(s_const, 16 * N_CONST)
                        nc.scalar.copy(id_b[:, :], id_f[:, :])
                        nc.scalar.copy(mask_b[:, :], mask_f[:, :]).then_inc(s_idb, 1)
                        act.wait_ge(s_vzero, 1)
                    if p is None and n == ("qs", 0):
                        act.wait_ge(s_sel_f, 16)
                        nc.scalar.copy(sel_sb[:, :, :, :], sel_f[:, :, :, :]).then_inc(s_sel, 1)
                    take(rd, n)
                for step in range(STEPS):
                    n_fill, piece = rd.filler(step)
                    if b is None:
                        if n_fill is not None:
                            take(rd, n_fill, piece)
                        continue
                    ss, ts, _, _, rt, _ = units_at(step)
                    for s in ss:
                        i, h = divmod(s, HEADS)
                        n = ("s", s)
                        act.wait_ge(s_max, b * UNITS + (s + 1))
                        if h == 0 and i >= 2:
                            act.wait_ge(s_rrep, b * TB + (i - 1))
                        taken(nc.scalar.activation(probs[:, s % 4, 0:(i + 1) * P], at(n, rd)[:, 0:(i + 1) * P], ACT.Exp,
                                                   bias=nmax[:, s % 8:s % 8 + 1], accum_out=rsum[:, i % 2, h:h + 1]),
                              n, rd)
                    for t in ts:
                        if on_act(t):
                            n = ("t", t)
                            w = (t // HEADS + 1) * P
                            filled(act, n, rd)
                            taken(nc.scalar.copy(probs_t[:, t % 4, 0:w], at(n, rd)[:, 0:w]), n, rd)
                    if rt is not None:
                        n = ("rt", rt)
                        filled(act, n, rd)
                        if rt > 0:
                            drained(act, ("pv", rt - 1), rd)
                        taken(nc.scalar.copy(rt_sb[:, :], at(n, rd)[:, 0:D]), n, rd)
                    if n_fill is not None:
                        take(rd, n_fill, piece)

            turn(Round(0))
            with act.Fori(1, B - 1) as b:
                turn(Round(b))
            turn(Round(B - 1))
            turn(Round(B))

            def gelu(j, z, g, s_z, s_g):
                act.wait_ge(s_z, j + 1)
                nc.scalar.activation(g[:, :], z[:, :], ACT.Gelu).then_inc(s_g, 1)

            def step(j, has):
                if has(2):
                    gelu(j + 2, z1, g1, s_z1, s_g1)
                if has(1):
                    gelu(j + 1, z2, g2, s_z2, s_g2)

            for j in (-2, -1):
                step(j, lambda d: 0 <= j + d)
            with act.Fori(0, TILES - 2) as j:
                step(j, lambda d: True)
            for j in range(TILES - 2, TILES):
                step(j, lambda d: j + d < TILES)

        @block.vector
        def _(dve):
            V = nc.vector
            dve.wait_ge(s_const, 16 * N_CONST)
            V.tensor_scalar(wq_raw[:, :, :].rearrange("p k n -> p (k n)"), wq_raw[:, :, :].rearrange("p k n -> p (k n)"),
                            DH ** -0.5, None, ALU.mult).then_inc(s_prep, 1)
            dve.sem_inc(s_hout, 1)

            def low_part(rd, n):
                what, m = n
                p = rd.p
                if what == "x1t":
                    dve.wait_ge(s_x_high, p * KD + (m + 1))
                    V.tensor_tensor(x_low[:, m, :], x1t[:, m, :], x_high[:, m, :].bitcast(F32), ALU.subtract
                                    ).then_inc(s_x_low, 1)
                elif what in ("fold_i", "fold_o"):
                    dve.wait_ge(s_eff_high, p * FOLDS + (fold_index(n) + 1))
                    if what == "fold_i":
                        cols = slice(m % 2 * 512, (m % 2 + 1) * 512)
                        low, high = wi_low[:, m // 2, cols], wi_high[:, m // 2, cols]
                    else:
                        low, high = (w[:, 2 * m:2 * m + 2, :].rearrange("p j d -> p (j d)") for w in (wf_low, wf_high))
                    taken(V.scalar_tensor_tensor(low, high.bitcast(F32), -1.0, at(n, rd)[:, :], ALU.mult, ALU.add),
                          n, rd)

            def take(rd, n, piece=None):
                what, m = n
                b, p = rd.b, rd.p
                if what in ("q", "k"):
                    slot = 0 if what == "q" else 2
                    dve.wait_ge(s_hi, b * (2 * KD) + (2 * m + slot // 2 + 1))
                    filled(dve, n, rd)
                    ins = V.scalar_tensor_tensor(parts[:, m, slot + 1, :], parts[:, m, slot, :].bitcast(F32), -1.0,
                                                 at(n, rd)[:, :], ALU.mult, ALU.add)
                elif what == "ks":
                    filled(dve, n, rd)
                    ins = V.tensor_copy(k_sb[:, m, :], at(n, rd)[:, :])
                elif what in ("fold_i", "fold_o"):
                    filled(dve, n, rd)
                    if what == "fold_i":
                        base = wi_base[:, m // 2, m % 2 * 512:(m % 2 + 1) * 512]
                    else:
                        base = wf_base[:, 2 * m:2 * m + 2, :].rearrange("p j d -> p (j d)")
                    V.scalar_tensor_tensor(at(n, rd)[:, :], at(n, rd)[:, :], 2.0, base, ALU.mult, ALU.add
                                           ).then_inc(s_eff, 1)
                    return
                elif what == "x1t":
                    if m == 0:
                        dve.wait_ge(s_xres, p * 16 + 16)
                    filled(dve, n, rd)
                    ins = V.tensor_tensor(x1t[:, m, :], at(n, rd)[:, :], x_res[:, m, :], ALU.add)
                elif what == "hid" and piece in (None, KD - 1):
                    dve.wait_ge(s_hid_high, p * KF + (m + 1))
                    ins = V.scalar_tensor_tensor(hid_low[:, m, :], at(n, rd)[:, :], 0.0,
                                                 hid_high[:, m, :].bitcast(F32), ALU.max, ALU.subtract)
                elif what == "h" and piece == H_PIECES - 1:
                    if m == 0:
                        dve.wait_ge(s_hout, p * 16 + 1)
                    filled(dve, n, rd)
                    ins = V.tensor_copy(h_sb[:, m, 0:D], at(n, rd)[:, 0:D])
                elif what == "ht" and m == 0:
                    filled(dve, n, rd)
                    ins = V.tensor_copy(ht_sb[:, 0, :], at(n, rd)[:, :])
                elif what == "gate":
                    filled(dve, n, rd)
                    taken(V.tensor_tensor(glog[:, :, :], at(n, rd)[:, 0:TB * NE].rearrange("p (t e) -> p t e", e=NE),
                                          gb_sb[:, :].unsqueeze(1).to_broadcast([P, TB, NE]), ALU.add), n, rd)
                    drained(dve, n, rd)
                    V.tensor_copy(logits[:, bass.ds(p * TB, TB), :], glog[:, :, :])
                    V.tensor_reduce(gmax[:, :], glog[:, :, :], AX.X, ALU.max).then_inc(s_gchain, 1)
                    dve.wait_ge(s_gchain, p * 3 + 1)
                    V.tensor_tensor(gexp[:, :, :], glog[:, :, :], gmax[:, :].unsqueeze(2).to_broadcast([P, TB, NE]),
                                    ALU.subtract).then_inc(s_gneg, 1)
                    return
                elif what == "softmax":
                    dve.wait_ge(s_gexp, p + 1)
                    V.tensor_reduce(gsum[:, :], gexp[:, :, :], AX.X, ALU.add).then_inc(s_gchain, 1)
                    dve.wait_ge(s_gchain, p * 3 + 2)
                    V.reciprocal(ginv[:, :], gsum[:, :]).then_inc(s_gchain, 1)
                    dve.wait_ge(s_gchain, p * 3 + 3)
                    V.tensor_tensor(h_sb[:, :, D:ROW], gexp[:, :, :], ginv[:, :].unsqueeze(2).to_broadcast([P, TB, NE]),
                                    ALU.mult).then_inc(s_hdone, 1)
                    return
                else:
                    return
                taken(ins, n, rd)

            def turn(rd):
                b, p = rd.b, rd.p
                for before, n in zip([None] + rd.opening, rd.opening + [None]):
                    if n is not None:
                        take(rd, n)
                    if before is not None:
                        low_part(rd, before)
                for step in range(STEPS):
                    n_fill, piece = rd.filler(step - 1) if step > 0 else (None, 0)
                    if b is None:
                        if n_fill is not None:
                            take(rd, n_fill, piece)
                        continue
                    ss, ts, _, inv, _, norm = units_at(step)
                    for s in ss:
                        n = ("s", s)
                        filled(dve, n, rd)
                        V.tensor_reduce(nmax[:, s % 8:s % 8 + 1], at(n, rd)[:, 0:(s // HEADS + 1) * P], AX.X, ALU.max,
                                        negate=True).then_inc(s_max, 1)
                    if norm is not None:
                        n = ("pv", norm)
                        drained(dve, ("rt", norm), rd)
                        filled(dve, n, rd)
                        taken(V.tensor_tensor(ot_sb[:, :, norm * P:(norm + 1) * P],
                                              at(n, rd)[:, 0:D].rearrange("p (k t) -> p k t", k=KD),
                                              rt_sb[:, :].rearrange("p (k t) -> p k t", k=KD), ALU.mult), n, rd)
                    for t in ts:
                        if not on_act(t):
                            n = ("t", t)
                            w = (t // HEADS + 1) * P
                            filled(dve, n, rd)
                            taken(V.tensor_copy(probs_t[:, t % 4, 0:w], at(n, rd)[:, 0:w]), n, rd)
                    if n_fill is not None:
                        take(rd, n_fill, piece)
                    if inv is not None:
                        drained(dve, ("s", inv * HEADS + HEADS - 1), rd)
                        V.reciprocal(rinv[:, :], rsum[:, inv % 2, :]).then_inc(s_chain, 1)
                        dve.wait_ge(s_chain, b * TB + (inv + 1))
                        V.tensor_copy(rrep[:, :].rearrange("p (h d) -> p h d", d=DH),
                                      rinv[:, :].unsqueeze(2).to_broadcast([P, HEADS, DH])).then_inc(s_rrep, 1)
                if p is not None:
                    take(rd, *rd.filler(STEPS - 1))

            turn(Round(0))
            dve.wait_ge(s_mid, 16 * N_MID)
            with dve.Fori(1, B - 1) as b:
                turn(Round(b))
            turn(Round(B - 1))
            turn(Round(B))

            links = [0]

            def link(ins):
                links[0] += 1
                ins.then_inc(s_rchain, 1)
                dve.wait_ge(s_rchain, links[0])

            def over_e(ap):
                return ap.unsqueeze(2).to_broadcast([P, NT, NE])

            for i in range(8):
                dve.wait_ge(full[i], before_b[i])
                dve.wait_ge(free[i], before_b[i] + 1)
            dve.wait_ge(s_rconst, 16 * N_RC)
            link(V.memset(ones_b[:, :], 1.0))
            link(V.tensor_copy(tri_sb[:, :], tri_f[:, :]))
            link(V.memset(etab[:, :, :], 0))
            link(V.memset(tbase[:, :], 0.0))
            for c in range(2):
                src = logits if c == 0 else lg2
                link(V.tensor_reduce(m1[:, :], src[:, :, :], AX.X, ALU.max))
                link(V.tensor_tensor(rk[:, :, :], src[:, :, :], over_e(m1[:, :]), ALU.is_equal))
                link(V.tensor_tensor(rk[:, :, :], rk[:, :, :],
                                     thr_sb[:, 2 * NT:2 * NT + NE].unsqueeze(1).to_broadcast([P, NT, NE]), ALU.mult))
                link(V.tensor_reduce(m1[:, :], rk[:, :, :], AX.X, ALU.max))
                link(V.tensor_tensor(hot[c][:, :, :], rk[:, :, :], over_e(m1[:, :]), ALU.is_equal))
                if c == 0:
                    link(V.scalar_tensor_tensor(lg2[:, :, :].rearrange("p t e -> p (t e)"),
                                                hot[0][:, :, :].rearrange("p t e -> p (t e)"), -BIG,
                                                logits[:, :, :].rearrange("p t e -> p (t e)"), ALU.mult, ALU.add))
            V.tensor_tensor(hots[:, :, :], hot[0][:, :, :], hot[1][:, :, :], ALU.add).then_inc(s_ohot, 1)
            dve.wait_ge(full[PRE_BANK], before_b[PRE_BANK] + 1)
            link(V.tensor_tensor(cmpt[:, :, :],
                                 bank[PRE_BANK][:, NT * NE:(NT + 1) * NE].unsqueeze(2).to_broadcast([P, NE, 2 * NT]),
                                 thr_sb[:, 0:2 * NT].unsqueeze(1).to_broadcast([P, NE, 2 * NT]), ALU.is_gt))
            link(V.tensor_reduce(ntile[:, :], cmpt[:, :, :], AX.X, ALU.add))
            for e in range(NE):
                link(V.tensor_tensor(tbase[:, e + 1:e + 2], tbase[:, e:e + 1], ntile[:, e:e + 1], ALU.add))
            V.scalar_tensor_tensor(pre[:, :, :], tbase[:, 0:NE].unsqueeze(1).to_broadcast([P, NT, NE]), float(P),
                                   bank[PRE_BANK][:, 0:NT * NE].rearrange("p (t e) -> p t e", e=NE),
                                   ALU.mult, ALU.add).then_inc(free[PRE_BANK], 1)
            dve.wait_ge(free[PRE_BANK], before_b[PRE_BANK] + 2)
            for c in range(2):
                link(V.tensor_tensor(rk[:, :, :], hot[c][:, :, :], pre[:, :, :], ALU.mult))
                link(V.tensor_reduce(slot[:, :], rk[:, :, :], AX.X, ALU.add))
                link(V.tensor_copy(s_i[:, 0, :], slot[:, :]))
                link(V.tensor_scalar(s_i[:, 1, :], s_i[:, 0, :], 7, None, ALU.arith_shift_right))
                link(V.tensor_copy(s_j[:, c, :], s_i[:, 1, :]))
                link(V.scalar_tensor_tensor(s_r[:, c, :], s_j[:, c, :], -float(P), slot[:, :], ALU.mult, ALU.add))
            for n in range(2 * NT // HIT_GROUP):
                c, t0 = divmod(n * HIT_GROUP, NT)
                if n >= 2:
                    dve.wait_ge(s_hitu, n - 1)
                V.tensor_tensor(hit_r[:, n % 2, :, :], iota_r_sb[:, :].unsqueeze(1).to_broadcast([P, HIT_GROUP, P]),
                                s_r[:, c, t0:t0 + HIT_GROUP].unsqueeze(2).to_broadcast([P, HIT_GROUP, P]),
                                ALU.is_equal).then_inc(s_hit_r, 1)
                if n >= 2:
                    dve.wait_ge(s_hit_v, n - 1)
                V.tensor_tensor(hit_j[:, n % 2, :, :], iota_t_sb[:, :].unsqueeze(1).to_broadcast([P, HIT_GROUP, TW]),
                                s_j[:, c, t0:t0 + HIT_GROUP].unsqueeze(2).to_broadcast([P, HIT_GROUP, TW]),
                                ALU.is_equal).then_inc(s_hit_j, 1)
            link(V.tensor_tensor(starts[:, :, :], iota_t_sb[0:1, 0:TILES].unsqueeze(2).to_broadcast([1, TILES, NE - 1]),
                                 tbase[0:1, 1:NE].unsqueeze(1).to_broadcast([1, TILES, NE - 1]), ALU.is_ge))
            link(V.tensor_reduce(expert_f[:, :], starts[:, :, :], AX.X, ALU.add))
            for d in range(AHEAD):
                link(V.tensor_copy(etab[:, 0:TILES - d, d], expert_f[:, d:TILES]))
            dve.wait_ge(s_hitu, 2 * NT // HIT_GROUP)
            V.tensor_copy(ids_g[:, :], bank[ID_BANK][:, 0:TILES]).then_inc(free[ID_BANK], 1)
            dve.wait_ge(free[ID_BANK], before_b[ID_BANK] + 2)
            link(V.tensor_scalar(ids_f[:, :], ids_g[:, :], -1.0, 0.0, ALU.add, ALU.max))
            link(V.tensor_copy(gather_id[:, :], ids_f[:, :]))
            link(V.tensor_scalar(ids_f[:, :], ids_g[:, :], 0.0, float(2 * B * S), ALU.is_equal, ALU.mult))
            link(V.scalar_tensor_tensor(ids_f[:, :], ids_g[:, :], -1.0, ids_f[:, :], ALU.add, ALU.add))
            V.tensor_copy(scatter_id[:, :], ids_f[:, :]).then_inc(s_route, 1)
            dve.wait_ge(s_route, 1)
            dve.wait_ge(s_bias, 16 * 3)

            e_regs = [dve.alloc_register(f"dve_expert{d}") for d in range(AHEAD)]

            def experts(j):
                dve.load(e_regs, etab[0:1, bass.ds(max(j, 0), 1) if isinstance(j, int) else bass.ds(j, 1), :]
                         .rearrange("p o d -> p (o d)"))
                e = [dve.snap(reg, min_val=0, max_val=NE - 1) for reg in e_regs]
                return [None] * -j + e if isinstance(j, int) and j < 0 else e

            def up(i, j):
                return before_c[i] + 1 + j

            def fl(i, j):
                return before_b[i] + (1 if i == PRE_BANK else 0) + 1 + j

            def x_evac(j, e):
                dve.wait_ge(s_xg, 16 * j + 16)
                V.tensor_copy(wsel[:, bass.ds(j, 1)], xg[:, bass.ds(e + D, 1)]).then_inc(s_wsel, 1)
                dve.wait_ge(full[BX], fl(BX, j))
                V.tensor_copy(xgt[:, :, :].rearrange("p k t -> p (k t)"), bank[BX][:, 0:D]).then_inc(free[BX], 1)

            def add_bias(j, e, bl, z, bias, s_z):
                dve.wait_ge(full[bl], fl(bl, j))
                V.tensor_tensor(z[:, :], bank[bl][:, :], bias[:, bass.ds(e, 1), :].rearrange("p o n -> p (o n)"),
                                ALU.add).then_inc(s_z, 1)

            def t_evac(j, bt, gt):
                dve.wait_ge(full[bt], fl(bt, j))
                V.tensor_copy(gt[:, :, :].rearrange("p k t -> p (k t)"), bank[bt][:, :]).then_inc(free[bt], 1)

            def first(d):
                return True

            def step(j, has):
                e = experts(j)
                if has(2):
                    add_bias(j + 2, e[2], BL1, z1, b1_sb, s_z1)
                if has(0):
                    t_evac(j, BT2, g2t)
                    dve.wait_ge(full[BL3], fl(BL3, j))
                    V.tensor_tensor(y0[:, :], bank[BL3][:, 0:D], b3_sb[:, bass.ds(e[0], 1), :].rearrange("p o n -> p (o n)"),
                                    ALU.add).then_inc(free[BL3], 1)
                    dve.wait_ge(free[BL3], up(BL3, j) + 1)
                    if has is not first:
                        dve.wait_ge(s_add, 16 * j)
                    V.tensor_scalar(y_sb[:, :], y0[:, :], wsel[:, bass.ds(j, 1)], None, ALU.mult).then_inc(s_y, 1)
                if has(3):
                    x_evac(j + 3, e[3])
                if has(1):
                    add_bias(j + 1, e[1], BL2, z2, b2_sb, s_z2)
                if has(2):
                    t_evac(j + 2, BT1, g1t)

            for j in (-3, -2, -1):
                step(j, lambda d: 0 <= j + d)
            step(0, first)
            with dve.Fori(1, TILES - 3) as j:
                step(j, lambda d: True)
            for j in range(TILES - 3, TILES):
                step(j, lambda d: j + d < TILES)

        @block.gpsimd
        def _(pool):
            nc.gpsimd.memset(v_sb[:, :, :, :, :, :].rearrange("p t s e a d -> p (t s e a d)"), 0.0).then_inc(s_vzero, 1)
            pool.wait_ge(s_rconst, 16 * N_RC)
            for n in range(2 * NT // HIT_GROUP):
                t0 = n * HIT_GROUP % NT
                pool.wait_ge(s_hit_j, n + 1)
                if n >= 2:
                    pool.wait_ge(s_hitu, n - 1)
                nc.gpsimd.tensor_tensor(hit_v[:, n % 2, :, :], hit_j[:, n % 2, :, :],
                                        tok_sb[:, t0:t0 + HIT_GROUP].unsqueeze(2).to_broadcast([P, HIT_GROUP, TW]),
                                        ALU.mult).then_inc(s_hit_v, 1)
            pool.wait_ge(s_route, 1)
            pool.wait_ge(s_hout, 16 * B + 1)
            pool.wait_ge(s_x1out, 16 * B + 1)

            def gather(j, vj1):
                nc.gpsimd.tensor_copy(gid[:, :], gather_id[:, bass.ds(j, 1)]).then_inc(s_gid, 1)
                pool.wait_ge(s_gid, vj1)
                pool.sem_inc(s_tick, 1)
                nc.gpsimd.indirect_dma_start(
                    xg[:, :], None, hrows, bass.IndirectOffsetOnAxis(ap=gid[:, 0:1], axis=0),
                    bounds_check=B * S - 1, oob_is_err=False).then_inc(s_xg, 16)

            def scatter(j, vj1):
                nc.gpsimd.tensor_copy(sid[:, :], scatter_id[:, bass.ds(j, 1)]).then_inc(s_sid, 1)
                pool.wait_ge(s_sid, vj1)
                pool.wait_ge(s_y, vj1)
                pool.sem_inc(s_tick, 1)
                nc.gpsimd.indirect_dma_start(
                    out_rows, bass.IndirectOffsetOnAxis(ap=sid[:, 0:1], axis=0), y_sb[:, :], None,
                    bounds_check=B * S - 1, oob_is_err=False, compute_op=ALU.add).then_inc(s_add, 16)

            def xg_free(v_bank, v_sel):
                pool.wait_ge(full[BX], v_bank)
                pool.sem_inc(s_tick, 1)
                pool.wait_ge(s_wsel, v_sel)
                pool.sem_inc(s_tick, 1)

            filled_x = before_b[BX] + b_uses[BX]
            gather(0, 1)
            for j in range(3):
                xg_free(filled_x + j + 1, j + 1)
                gather(j + 1, j + 2)
            scatter(0, 1)
            xg_free(filled_x + 4, 4)
            gather(4, 5)
            with pool.Fori(1, TILES - 4) as j:
                v_added, v_j1, v_j4, v_j5 = (pool.snap(v) for v in (16 * j, j + 1, j + 4, j + 5))
                v_bx = pool.snap(j + (filled_x + 4))
                pool.wait_ge(s_add, v_added)
                scatter(j, v_j1)
                xg_free(v_bx, v_j4)
                gather(v_j4, v_j5)
            for j in range(TILES - 4, TILES):
                pool.wait_ge(s_add, 16 * j)
                scatter(j, j + 1)


_OUTS = [((B, S, D), "float32")]


def kernel(**inputs):
    import numpy as _np
    import concourse.bacc as _bacc
    from concourse import mybir as _mybir
    from concourse.bass_utils import run_bass_kernel_spmd as _run

    def chunked(w):
        n, k, m = w.shape
        return w.reshape(n, k // P, P, m).transpose(0, 2, 1, 3)

    def get(name):
        return _np.asarray(inputs[name])

    def lora_rows(wi_a, wi_b, wo_a, wo_b):
        return _np.concatenate([wi_a, wi_b.swapaxes(-1, -2), wo_a, wo_b.swapaxes(-1, -2)], axis=-1)

    iota = _np.arange(P, dtype=_np.float32)
    data = {
        "xT": chunked(get("x").transpose(0, 2, 1)),
        "cond_w": chunked(get("L0_cond_weight").transpose(0, 2, 1)),
        "cond_b": get("L0_cond_bias").reshape(NE, KD, P).transpose(0, 2, 1),
        "itok": get("itok_B_0_7").reshape(1, B),
        "wq": chunked(get("L0_attn_W_Q")[None])[0],
        "wk": chunked(get("L0_attn_W_K")[None])[0],
        "wv": chunked(get("L0_attn_W_V")[None])[0],
        "wo": chunked(get("L0_attn_W_o")[None])[0],
        "wi_t": chunked(get("L0_cond2_wi").T[None])[0],
        "wo_t": chunked(get("L0_cond2_wo").T[None])[0],
        "lora_c": lora_rows(*(get("L0_cond2_common_" + n) for n in ("wi_a", "wi_b", "wo_a", "wo_b"))),
        "lora_e": lora_rows(*(get("L0_cond2_experts_" + n) for n in ("wi_a", "wi_b", "wo_a", "wo_b"))),
        "gate_w": chunked(get("L0_ffn_gate_w")[None])[0],
        "gate_b": get("L0_ffn_gate_b").reshape(NE),
        "w1": chunked(get("L0_ffn_w1")),
        "w2": chunked(get("L0_ffn_w2")),
        "w3": chunked(get("L0_ffn_w3")),
        "b1": get("L0_ffn_b1").reshape(NE * H),
        "b2": get("L0_ffn_b2").reshape(NE * H),
        "b3": get("L0_ffn_b3").reshape(NE * D),
        "ident": _np.eye(P, dtype=_np.float32),
        "maskd": _np.triu(_np.full((P, P), -BIG, _np.float32), 1),
        "tri": _np.triu(_np.ones((P, P), _np.float32), 1),
        "sel": _np.stack([_np.stack([_np.kron(_np.eye(4)[:, pair:pair + 1], _np.kron(_np.eye(2),
                                              _np.kron(rows, _np.eye(DH)))) for pair in range(4)], axis=1)
                          for rows in ([[1, 0, 1, 0]], [[0, 1, 0, 1]], [[1, 1, 0, 0]], [[0, 0, 1, 1]])],
                         axis=1).astype(_np.float32),
        "iota_r": _np.tile(iota, (P, 1)),
        "iota_t": _np.tile(_np.arange(TW, dtype=_np.float32), (P, 1)),
        "tok": (_np.arange(NT)[None, :] * P + _np.arange(P)[:, None] + 1).astype(_np.float32),
        "thr": _np.tile(_np.concatenate([_np.arange(2 * NT) * P, NE - _np.arange(NE)]).astype(_np.float32), (P, 1)),
    }
    nc = _bacc.Bacc("TRN2", target_bir_lowering=False, num_devices=1)
    arrays, args = {}, []
    for name, a in data.items():
        a = _np.ascontiguousarray(a)
        arrays[f"in_{name}"] = a
        args.append(nc.dram_tensor(f"in_{name}", a.shape, _mybir.dt.from_np(a.dtype), kind="ExternalInput").ap())
    for i, (shape, dtype) in enumerate(_OUTS):
        dt = _mybir.dt.from_np(_np.dtype(dtype))
        args.append(nc.dram_tensor(f"out_{i}", shape, dt, kind="ExternalOutput").ap())
    build_kernel(nc, *args)
    r = _run(nc, [arrays], core_ids=[0])
    return r.results[0]["out_0"]
```
